# Optimizing a Trainium2 kernel written in Bass

```python
import numpy as np
import jax
import jax.numpy as jnp

def _softmax(x, axis=-1):
    return jax.nn.softmax(x, axis=axis)

def _gelu(x):
    return jax.nn.gelu(x, approximate=True)

def _silu(x):
    return jax.nn.silu(x)

def _sigmoid(x):
    return jax.nn.sigmoid(x)

def _layernorm(x, axis=-1, eps=1e-05):
    m = jnp.mean(x, axis=axis, keepdims=True)
    v = jnp.var(x, axis=axis, keepdims=True)
    return (x - m) / jnp.sqrt(v + eps)

def _scatter_add(tgt, idx, src, axis=0):
    return tgt.at[idx].add(src)

def _segment_sum(src, seg, n):
    return jax.ops.segment_sum(src, seg, n)
kernel_name = 'mk_gnn_resnorm_d4_gnn_r8_49c298'

def setup_inputs(seed: int=0):
    np.random.seed(seed)
    _w = jnp.asarray

    def _rec_inputs():
        import jax
        import jax.numpy as jnp
        _gk = jax.random.key(seed)
        x = -0.0005121 + 1.001 * jax.random.normal(jax.random.fold_in(_gk, 1), (12500, 32), jnp.float32)
        _s = jax.random.randint(jax.random.fold_in(_gk, 2), (200000,), 0, 12500, jnp.int32)
        _d = jax.random.randint(jax.random.fold_in(_gk, 3), (200000,), 0, 12500, jnp.int32)
        _loop = jnp.arange(12500, dtype=jnp.int32)
        src = jnp.concatenate([_s, _d, _loop])
        dst = jnp.concatenate([_d, _s, _loop])
        _o = jnp.argsort(dst, stable=True)
        src = src[_o]
        dst = dst[_o]
        edge_attr_32 = -8.16379e-05 + 0.999858 * jax.random.normal(jax.random.fold_in(_gk, 12), (412500, 32), jnp.float32)
        edge_weight = jax.random.uniform(jax.random.fold_in(_gk, 14), (412500,), jnp.float32, 0.0, 1)
        return (x, src, dst, edge_attr_32, edge_weight)
    x, src, dst, edge_attr_32, edge_weight = _rec_inputs()

    def _L0_gnn_setup():
        import jax, jax.numpy as jnp
        import numpy as np
        N_NODES = 12500
        N_EDGES = 200000
        D_FEAT = 32
        key = jax.random.key(seed)
        k1, k2, k3 = jax.random.split(key, 3)
        features = jax.random.normal(k1, (N_NODES, D_FEAT), dtype=jnp.float32)
        src = jax.random.randint(k2, (N_EDGES,), 0, N_NODES, dtype=jnp.int64)
        dst = jax.random.randint(k3, (N_EDGES,), 0, N_NODES, dtype=jnp.int64)
        return {'features': features, 'src': src, 'dst': dst}
    _L0_gnn_all = _L0_gnn_setup()
    _L0_gnn_in = {k: v for k, v in _L0_gnn_all.items() if k in ()}
    del _L0_gnn_all

    def _L1_gnn_setup():
        import jax, jax.numpy as jnp
        import numpy as np
        N_NODES = 12500
        N_EDGES = 400000
        D = 32
        N_LAYERS = 5

        def _gine_layer(x, edge_attr, src, dst, eps_l, W1_l, b1_l, W2_l, b2_l, n_nodes):
            msg = jax.nn.relu(x[src] + edge_attr)
            agg = jax.ops.segment_sum(msg, dst, num_segments=n_nodes)
            h = (1.0 + eps_l) * x + agg
            h = jax.nn.relu(h @ W1_l.T + b1_l)
            return h @ W2_l.T + b2_l
        key = jax.random.key(seed)
        ks = jax.random.split(key, 8)
        x = jax.random.normal(ks[0], (N_NODES, D), dtype=jnp.float32)
        edge_attr = jax.random.normal(ks[1], (N_EDGES, D), dtype=jnp.float32)
        edge_index = jax.random.randint(ks[2], (2, N_EDGES), 0, N_NODES, dtype=jnp.int64)
        eps = jnp.zeros((N_LAYERS,), dtype=jnp.float32)
        scale = 1.0 / np.sqrt(D)
        W1 = jax.random.normal(ks[3], (N_LAYERS, D, D), dtype=jnp.float32) * scale
        b1 = jax.random.normal(ks[4], (N_LAYERS, D), dtype=jnp.float32) * scale
        W2 = jax.random.normal(ks[5], (N_LAYERS, D, D), dtype=jnp.float32) * scale
        b2 = jax.random.normal(ks[6], (N_LAYERS, D), dtype=jnp.float32) * scale
        return {'x': x, 'edge_attr': edge_attr, 'eps': eps, 'W1': W1, 'b1': b1, 'W2': W2, 'b2': b2, 'edge_index': edge_index}
    _L1_gnn_all = _L1_gnn_setup()
    _L1_gnn_in = {k: v for k, v in _L1_gnn_all.items() if k in ('eps', 'W1', 'b1', 'W2', 'b2')}
    del _L1_gnn_all

    def _L2_gnn_setup():
        import jax, jax.numpy as jnp
        import numpy as np
        N_NODES = 12500
        N_EDGES = 200000
        F_IN = 32
        F_OUT = 32
        key = jax.random.key(seed)
        kx, kr, kc, kv, kw = jax.random.split(key, 5)
        x = jax.random.normal(kx, (N_NODES, F_IN), dtype=jnp.float32)
        rows = jnp.sort(jax.random.randint(kr, (N_EDGES,), 0, N_NODES, dtype=jnp.int64))
        cols = jax.random.randint(kc, (N_EDGES,), 0, N_NODES, dtype=jnp.int64)
        vals = jax.random.uniform(kv, (N_EDGES,), dtype=jnp.float32)
        weight = jax.random.normal(kw, (F_IN, F_OUT), dtype=jnp.float32) / np.sqrt(F_IN)
        return {'x': x, 'rows': rows, 'cols': cols, 'vals': vals, 'weight': weight}
    _L2_gnn_all = _L2_gnn_setup()
    _L2_gnn_in = {k: v for k, v in _L2_gnn_all.items() if k in ('weight',)}
    del _L2_gnn_all

    def _L3_gnn_setup():
        import jax, jax.numpy as jnp
        import numpy as np
        N_NODES = 12500
        N_EDGES = 250000
        C = 32
        key = jax.random.key(seed)
        k1, k2, k3, k4 = jax.random.split(key, 4)
        x = jax.random.normal(k1, (N_NODES, C), dtype=jnp.float32)
        edge_index = jax.random.randint(k2, (2, N_EDGES), 0, N_NODES, dtype=jnp.int64)
        initrange = 0.1
        w_src = jax.random.uniform(k3, (C,), dtype=jnp.float32, minval=-initrange, maxval=initrange)
        w_tgt = jax.random.uniform(k4, (C,), dtype=jnp.float32, minval=-initrange, maxval=initrange)
        gate_bias = jnp.zeros((1,), dtype=jnp.float32)
        return {'x': x, 'edge_index': edge_index, 'w_src': w_src, 'w_tgt': w_tgt, 'gate_bias': gate_bias}
    _L3_gnn_all = _L3_gnn_setup()
    _L3_gnn_in = {k: v for k, v in _L3_gnn_all.items() if k in ('w_src', 'w_tgt', 'gate_bias')}
    del _L3_gnn_all
    return {'x': x, 'src': src, 'dst': dst, 'edge_attr_32': edge_attr_32, 'edge_weight': edge_weight, 'L1_gnn_eps': _L1_gnn_in['eps'], 'L1_gnn_W1': _L1_gnn_in['W1'], 'L1_gnn_b1': _L1_gnn_in['b1'], 'L1_gnn_W2': _L1_gnn_in['W2'], 'L1_gnn_b2': _L1_gnn_in['b2'], 'L2_gnn_weight': _L2_gnn_in['weight'], 'L3_gnn_w_src': _L3_gnn_in['w_src'], 'L3_gnn_w_tgt': _L3_gnn_in['w_tgt'], 'L3_gnn_gate_bias': _L3_gnn_in['gate_bias']}

def reference(x, src, dst, edge_attr_32, edge_weight, L1_gnn_eps, L1_gnn_W1, L1_gnn_b1, L1_gnn_W2, L1_gnn_b2, L2_gnn_weight, L3_gnn_w_src, L3_gnn_w_tgt, L3_gnn_gate_bias):
    import jax
    import jax.numpy as jnp

    def _L0_gnn_ref(features, src, dst):
        import jax, jax.numpy as jnp
        import numpy as np
        N_NODES = 12500
        N_EDGES = 200000
        D_FEAT = 32
        messages = features[src]
        h = jax.ops.segment_sum(messages, dst, num_segments=N_NODES)
        return h

    def _L1_gnn_ref(x, edge_attr, eps, W1, b1, W2, b2, edge_index):
        import jax, jax.numpy as jnp
        import numpy as np
        N_NODES = 12500
        N_EDGES = 400000
        D = 32
        N_LAYERS = 5

        def _gine_layer(x, edge_attr, src, dst, eps_l, W1_l, b1_l, W2_l, b2_l, n_nodes):
            msg = jax.nn.relu(x[src] + edge_attr)
            agg = jax.ops.segment_sum(msg, dst, num_segments=n_nodes)
            h = (1.0 + eps_l) * x + agg
            h = jax.nn.relu(h @ W1_l.T + b1_l)
            return h @ W2_l.T + b2_l
        src = edge_index[0]
        dst = edge_index[1]
        n_nodes = x.shape[0]
        out = x
        for l in range(N_LAYERS):
            out = jax.nn.relu(_gine_layer(x, edge_attr, src, dst, eps[l], W1[l], b1[l], W2[l], b2[l], n_nodes))
        return out

    def _L2_gnn_ref(x, rows, cols, vals, weight):
        import jax, jax.numpy as jnp
        import numpy as np
        N_NODES = 12500
        N_EDGES = 200000
        F_IN = 32
        F_OUT = 32
        gathered = x[cols] * vals[:, None]
        z = jax.ops.segment_sum(gathered, rows, num_segments=x.shape[0])
        return z @ weight

    def _L3_gnn_ref(x, edge_index, w_src, w_tgt, gate_bias):
        import jax, jax.numpy as jnp
        import numpy as np
        N_NODES = 12500
        N_EDGES = 250000
        C = 32
        N = x.shape[0]
        src = edge_index[0]
        dst = edge_index[1]
        ones = jnp.ones(src.shape[0], dtype=x.dtype)
        deg = jax.ops.segment_sum(ones, src, num_segments=N)
        deg_inv_sqrt = jnp.where(deg > 0, deg ** (-0.5), 0.0)
        norm = deg_inv_sqrt[src] * deg_inv_sqrt[dst]
        x_j = x[src]
        x_i = x[dst]
        gate = jax.nn.sigmoid(x_j @ w_src + x_i @ w_tgt + gate_bias[0])
        msg = (norm * gate)[:, None] * x_j
        out = jax.ops.segment_sum(msg, dst, num_segments=N)
        return out
    edge_index = jnp.stack([src, dst])
    x = _layernorm(x + _L0_gnn_ref(x, src, dst), axis=-1)
    x = _layernorm(x + _L1_gnn_ref(x, edge_attr_32, L1_gnn_eps, L1_gnn_W1, L1_gnn_b1, L1_gnn_W2, L1_gnn_b2, edge_index), axis=-1)
    x = _layernorm(x + _L2_gnn_ref(x, src, dst, edge_weight, L2_gnn_weight), axis=-1)
    x = _layernorm(x + _L3_gnn_ref(x, edge_index, L3_gnn_w_src, L3_gnn_w_tgt, L3_gnn_gate_bias), axis=-1)
    return x

_drawn_inputs = setup_inputs


def setup_inputs(seed=0):
    import zlib

    import numpy as np

    out = dict(_drawn_inputs(seed))
    spreads = {'L1_gnn_eps': (0.0, 0.8)}
    factors = {'L1_gnn_b1': 8.0, 'L1_gnn_b2': 2.786, 'L3_gnn_w_src': 8.0, 'L3_gnn_w_tgt': 8.0}
    for name, (base, spread) in spreads.items():
        noise = np.random.default_rng([zlib.crc32(name.encode()), seed]).standard_normal(out[name].shape)
        drawn = base * np.exp(spread * noise) if base else spread * noise
        out[name] = jnp.asarray(drawn.astype(out[name].dtype))
    for name, factor in factors.items():
        out[name] = (out[name] * factor).astype(out[name].dtype)
    return out
```

```python
from contextlib import ExitStack

import concourse.bass as bass
from concourse import mybir

F32 = mybir.dt.float32
BF16 = mybir.dt.bfloat16
I32 = mybir.dt.int32
ALU = mybir.AluOpType
ACT = mybir.ActivationFunctionType
X = mybir.AxisListType.X

P = 128
K = 12
SUPER = K * P
W = 64
LOG_W = 6
R = 4
BANK = 512
EPS = 1e-5


class Tile:

    def __init__(self, number, turn, slot, rows, first):
        self.number, self.turn, self.slot, self.rows, self.first = number, turn, slot, rows, first


def build_program(nc, x, src, dst, edge_attr, edge_weight, eps, w1, b1, w2, b2, w_lin, w_src, w_tgt,
                  gate_bias, out):
    N, D = x.shape
    E = src.shape[0]
    L = eps.shape[0]
    B = -(-N // P)
    NP = P * B
    NT = -(-max(NP + W, N + P) // P) * P
    FULL = E // SUPER
    TAIL = (E - FULL * SUPER) // K
    TILES = FULL + 1
    PAIRS = FULL // 2
    assert FULL % 2 == 0 and E == FULL * SUPER + TAIL * K and 0 < TAIL < P and D == 32
    WINDOWS = -(-N // W) + 1
    MOST = TILES * WINDOWS
    CHUNKS = -(-TILES // P)
    HI = -(-N // P)
    YC = 36
    LASTROWS = N - (P - 1) * B

    def node_rows(table, cols=D):
        return table[0:NP, :].rearrange("(p b) f -> p (b f)", b=B)

    src_rows = src.rearrange("(r k) -> r k", k=K)
    dst_rows = dst.rearrange("(r k) -> r k", k=K)
    weight_rows = edge_weight.rearrange("(r k) -> r k", k=K)
    attr_rows = edge_attr.rearrange("(r k) f -> r (k f)", k=K)

    x1_dram = nc.dram_tensor("x1_table", (NT, D), F32, kind="Internal").ap()
    x2_dram = nc.dram_tensor("x2_table", (NT, D), F32, kind="Internal").ap()
    y_dram = nc.dram_tensor("y_table", (NT, YC), F32, kind="Internal").ap()
    z_dram = [nc.dram_tensor(f"z_part{r}", (NT, D), F32, kind="Internal").ap() for r in range(R)]
    b_dram = nc.dram_tensor("target_logit", (NT, 1), F32, kind="Internal").ap()
    deg_dram = nc.dram_tensor("degree", (HI, P), F32, kind="Internal").ap()
    win_dram = nc.dram_tensor("window_table", (CHUNKS * P, 4), I32, kind="Internal").ap()
    base_dram = nc.dram_tensor("window_base", (CHUNKS * P, 1), F32, kind="Internal").ap()

    with ExitStack() as ctx:
        def sb(name, shape, dt=F32, scope=ctx):
            return scope.enter_context(nc.sbuf_tensor(name, shape, dt))

        iota_w = sb("iota_w", [P, W])
        iota_hi = sb("iota_hi", [P, HI])
        iota_lo = sb("iota_lo", [P, P])
        window_off = sb("window_off", [P, WINDOWS])
        window_node = sb("window_node", [P, WINDOWS])
        dump_row = sb("dump_row", [P, 1])
        ident = sb("ident", [P, P])
        before = sb("before", [P, P])
        below = sb("below", [P, P])
        ones = sb("ones", [P, P])
        eps_col = sb("eps_col", [P, 1])
        windows = sb("windows", [1, TILES * 4], I32)
        base_all = sb("base_all", [P, TILES])
        xs = sb("xs", [P, B, D])
        hs = sb("hs", [P, B, D])
        tmp = sb("tmp", [P, B, D])
        agg = sb("agg", [D, NP + W])
        stat = sb("stat", [P, B])
        dis = sb("dis", [P, B])

        def super_tiles(eng):
            for slot in (0, 1):
                yield Tile(slot, 0, slot, P, True)
            with eng.Fori(1, PAIRS) as i:
                for slot in (0, 1):
                    yield Tile(2 * i + slot, i, slot, P, False)
            yield Tile(2 * PAIRS, PAIRS, 0, TAIL, False)

        def window_range(eng, tile):
            first = eng.value_load(windows[0:1, bass.ds(4 * tile.number, 1)], min_val=0, max_val=MOST)
            end = eng.value_load(windows[0:1, bass.ds(4 * tile.number + 1, 1)], min_val=1, max_val=MOST)
            base = eng.value_load(windows[0:1, bass.ds(4 * tile.number + 2, 1)],
                                  min_val=-W * MOST, max_val=N)
            return first, end, base

        passed = ctx.enter_context(nc.semaphore("passed"))

        def wait_alone(eng, semaphore, value):
            eng.wait_ge(semaphore, value)
            eng.sem_inc(passed, 1)

        def first_node(base, j):
            return (base + W * j).with_bounds(min_val=0, max_val=NP)

        def edge_rows(rows, tile):
            return rows[bass.ds(tile.number * P, tile.rows), :]

        with ExitStack() as ph:
            sem = lambda name: ph.enter_context(nc.semaphore(name))
            dst_tiles = sb("dst_tiles", [P, CHUNKS, SUPER], I32, ph)
            low = sb("low", [P, CHUNKS], F32, ph)
            high = sb("high", [P, CHUNKS], F32, ph)
            span = sb("span", [P, CHUNKS], I32, ph)
            count = sb("count", [P, CHUNKS], F32, ph)
            start = sb("start", [P, CHUNKS], F32, ph)
            table = sb("table", [P, CHUNKS, 4], I32, ph)
            prefix = ph.enter_context(nc.psum_tensor("prefix", [P, 2, 4], F32))
            dst_in, x_in, filled, made, spans, prefixed, table_made = (
                sem("dst_in"), sem("x_in"), sem("filled"), sem("made"), sem("spans"), sem("prefixed"),
                sem("table_made"))
            table_out, windows_in, zeroed, cleared = (
                sem("table_out"), sem("windows_in"), sem("zeroed"), sem("cleared"))
            last = TILES - 1 - (CHUNKS - 1) * P
            block = ph.enter_context(nc.Block())

            @block.sync
            def _(sp):
                for c in range(CHUNKS - 1):
                    sp.dma_start(dst_tiles[:, c, :],
                                 dst[c * P * SUPER:(c + 1) * P * SUPER]
                                 .rearrange("(t e) -> t e", e=SUPER)).then_inc(dst_in, 16)
                sp.dma_start(dst_tiles[0:last, CHUNKS - 1, :],
                             dst[(CHUNKS - 1) * P * SUPER:FULL * SUPER]
                             .rearrange("(t e) -> t e", e=SUPER)).then_inc(dst_in, 16)
                sp.dma_start(dst_tiles[last:last + 1, CHUNKS - 1, :],
                             dst[E - SUPER:E].rearrange("(t e) -> t e", e=SUPER)).then_inc(dst_in, 16)
                sp.wait_ge(filled, 1)
                sp.dma_start(xs[0:P - 1, :, :].rearrange("p b f -> p (b f)"),
                             x[0:(P - 1) * B, :].rearrange("(p b) f -> p (b f)", b=B)).then_inc(x_in, 16)
                sp.dma_start(xs[P - 1:P, 0:LASTROWS, :].rearrange("p b f -> p (b f)"),
                             x[(P - 1) * B:N, :].rearrange("(p b) f -> p (b f)", b=LASTROWS)
                             ).then_inc(x_in, 16)
                sp.wait_ge(cleared, 1)
                for r in range(R):
                    sp.dma_start(node_rows(z_dram[r]), hs[:, :, :].rearrange("p b f -> p (b f)")
                                 ).then_inc(zeroed, 16)
                    sp.dma_start(z_dram[r][NP:NT, :], hs[0:NT - NP, 0, :]).then_inc(zeroed, 16)
                sp.dma_start(x2_dram[NP:NT, :], hs[0:NT - NP, 0, :]).then_inc(zeroed, 16)
                sp.dma_start(b_dram[NP:NT, :], hs[0:NT - NP, 0, 0:1]).then_inc(zeroed, 16)
                sp.wait_ge(table_made, 2)
                sp.dma_start(win_dram.rearrange("(c p) q -> p c q", p=P), table[:, :, :]
                             ).then_inc(table_out, 16)
                with nc.allow_non_contiguous_dma(reason="one word per tile"):
                    sp.dma_start(base_dram.rearrange("(c p) q -> p (c q)", p=P), low[:, :]
                                 ).then_inc(table_out, 16)
                sp.wait_ge(table_out, 32)
                sp.dma_start(windows[:, :], win_dram[0:TILES, :].rearrange("t q -> (t q)")
                             .rearrange("(a n) -> a n", a=1)).then_inc(windows_in, 16)
                sp.dma_start(base_all[:, :], base_dram[0:TILES, :].rearrange("t q -> q t")
                             .to_broadcast([P, TILES])).then_inc(windows_in, 16)
                sp.wait_ge(windows_in, 32)
                sp.wait_ge(zeroed, 16 * (2 * R + 2))
                sp.wait_ge(x_in, 32)

            @block.gpsimd
            def _(pool):
                pool.memset(xs[:, :, :], 0.0).then_inc(filled, 1)
                pool.memset(ident[:, :], 0.0).then_inc(made, 1)
                pool.memset(ones[:, :], 1.0).then_inc(made, 1)
                pool.wait_ge(made, 2)
                pool.affine_select(out=ident[:, :], in_=ident[:, :], compare_op=ALU.not_equal, fill=1.0,
                                   base=0, pattern=[[-1, P]], channel_multiplier=1)
                pool.affine_select(out=before[:, :], in_=ones[:, :], compare_op=ALU.is_gt, fill=0.0,
                                   base=0, pattern=[[-1, P]], channel_multiplier=1)
                pool.affine_select(out=below[:, :], in_=ones[:, :], compare_op=ALU.is_gt, fill=0.0,
                                   base=0, pattern=[[1, P]], channel_multiplier=-1).then_inc(made, 1)
                for tile, step, num, base, mult in ((iota_w, 1, W, 0, 0), (iota_hi, 1, HI, 0, 0),
                                                    (iota_lo, 1, P, 0, 0), (window_off, W, WINDOWS, 0, 0),
                                                    (window_node, W, WINDOWS, 0, 1), (dump_row, 1, 1, N, 1)):
                    pool.iota(tile[:, :], pattern=[[step, num]], base=base, channel_multiplier=mult,
                              allow_small_or_imprecise_dtypes=True)

            @block.vector
            def _(dve):
                nc.vector.memset(hs[:, :, :], 0.0).then_inc(cleared, 1)
                nc.vector.memset(agg[:, :], 0.0)
                nc.vector.memset(eps_col[:, :], EPS)
                nc.vector.memset(low[:, :], 0.0)
                nc.vector.memset(high[:, :], 0.0)
                nc.vector.memset(table[:, :, :], 0)
                dve.wait_ge(dst_in, 16 * (CHUNKS + 1))
                dve.drain()
                for c in range(CHUNKS):
                    rows = P if c < CHUNKS - 1 else last + 1
                    nc.vector.tensor_reduce(low[0:rows, c:c + 1], dst_tiles[0:rows, c, :], X, ALU.min)
                    nc.vector.tensor_reduce(high[0:rows, c:c + 1], dst_tiles[0:rows, c, :], X, ALU.max)
                dve.drain()
                nc.vector.tensor_tensor(span[:, :], high[:, :], low[:, :], ALU.subtract)
                dve.drain()
                nc.vector.tensor_scalar(span[:, :], span[:, :], LOG_W, None, ALU.arith_shift_right)
                dve.drain()
                nc.vector.tensor_scalar(count[:, :], span[:, :], 1.0, None, ALU.add).then_inc(spans, 1)
                dve.wait_ge(prefixed, 1)
                nc.vector.tensor_copy(start[:, :], prefix[:, 0, 0:CHUNKS])
                for c in range(CHUNKS - 1):
                    for later in range(c + 1, CHUNKS):
                        dve.drain()
                        nc.vector.tensor_tensor(start[:, later:later + 1], start[:, later:later + 1],
                                                prefix[:, 1, c:c + 1], ALU.add)
                dve.drain()
                nc.vector.tensor_copy(table[:, :, 0], start[:, :])
                nc.vector.tensor_tensor(table[:, :, 1], start[:, :], count[:, :], ALU.add)
                dve.drain()
                nc.vector.tensor_scalar(count[:, :], start[:, :], -float(W), None, ALU.mult)
                dve.drain()
                nc.vector.tensor_tensor(table[:, :, 2], count[:, :], low[:, :], ALU.add)
                dve.drain().then_inc(table_made, 2)

            @block.tensor
            def _(pe):
                pe.wait_ge(spans, 1)
                pe.wait_ge(made, 3)
                nc.tensor.matmul(prefix[:, 0, 0:CHUNKS], below[:, :], count[:, :], start=True, stop=True)
                nc.tensor.matmul(prefix[:, 1, 0:CHUNKS], ones[:, :], count[:, :], start=True, stop=True
                                 ).then_inc(prefixed, 1)

        def sum_by_dst(layer):
            cols = YC if layer == 3 else D
            node_table = {0: x, 1: x1_dram[0:NP, :], 3: y_dram[0:NP, :]}[layer]
            with ExitStack() as ph:
                sem = lambda name: ph.enter_context(nc.semaphore(f"{name}{layer}"))
                buf = lambda name, shape, dt=F32: sb(f"{name}{layer}", shape, dt, ph)
                psum = lambda name, shape: ph.enter_context(nc.psum_tensor(f"{name}{layer}", shape, F32))
                src_idx = buf("src_idx", [P, 2, K], I32)
                dst_idx = buf("dst_idx", [P, 2, K], I32)
                got = buf("got", [P, 2, K, cols])
                rel = buf("rel", [P, K])
                pick = buf("pick", [P, K, W])
                sums = psum("sums", [D, BANK])
                edges_in = [sem(f"edges_in{s}_") for s in (0, 1)]
                gathered = [sem(f"gathered{s}_") for s in (0, 1)]
                tile_done = [sem(f"tile_done{s}_") for s in (0, 1)]
                pick_made, summed = sem("pick_made"), sem("summed")
                if layer == 0:
                    digit = buf("digit", [P, 2, K], I32)
                    hot_hi = buf("hot_hi", [P, K, HI], BF16)
                    hot_lo = buf("hot_lo", [P, K, P], BF16)
                    degree = psum("degree_ps", [P, BANK])
                    degree_turned_ps = psum("degree_turned_ps", [P, BANK])
                    digits_made, counted, degree_copied, degree_turned, turned_copied, degree_out, dis_in = (
                        sem("digits_made"), sem("counted"), sem("degree_copied"), sem("degree_turned"),
                        sem("turned_copied"), sem("degree_out"), sem("dis_in"))
                    degree_lo = buf("degree_lo", [P, HI])
                    degree_hi = buf("degree_hi", [HI, P])
                if layer == 1:
                    attr = buf("attr", [P, 2, K * D])
                    attr_in = [sem(f"attr_in{s}_") for s in (0, 1)]
                    added, rectified = sem("added"), sem("rectified")
                if layer == 3:
                    target = buf("target", [P, W])
                    share = buf("share", [P, K, W])
                    logit = buf("logit", [P, K])
                    gate = buf("gate", [P, K])
                    msg = buf("msg", [P, K, D])
                    target_in, target_used, logits_made, gated, msg_made = (
                        sem("target_in"), sem("target_used"), sem("logits_made"), sem("gated"),
                        sem("msg_made"))
                block = ph.enter_context(nc.Block())

                @block.sync
                def _(sp):
                    for t in super_tiles(sp):
                        if not t.first:
                            sp.wait_ge(tile_done[t.slot], t.turn)
                        sp.dma_start(src_idx[0:t.rows, t.slot, :], edge_rows(src_rows, t)
                                     ).then_inc(edges_in[t.slot], 16)
                        sp.dma_start(dst_idx[0:t.rows, t.slot, :], edge_rows(dst_rows, t)
                                     ).then_inc(edges_in[t.slot], 16)
                        if layer == 1:
                            sp.dma_start(attr[0:t.rows, t.slot, :], edge_rows(attr_rows, t)
                                         ).then_inc(attr_in[t.slot], 16)
                        if layer == 3:
                            first, end, base = window_range(sp, t)
                            with sp.Fori(first, end) as j:
                                sp.wait_ge(target_used, j + 1)
                                sp.dma_start(target[:, :], b_dram[bass.ds(first_node(base, j), W), :]
                                             .rearrange("n q -> q n").to_broadcast([P, W])
                                             ).then_inc(target_in, 16)
                    if layer == 0:
                        sp.wait_ge(turned_copied, 1)
                        sp.dma_start(deg_dram, degree_hi[:, :]).then_inc(degree_out, 16)
                        sp.wait_ge(degree_out, 16)
                        sp.dma_start(dis[:, :], deg_dram.rearrange("h l -> (h l)")
                                     .rearrange("(p b) -> p b", b=B)).then_inc(dis_in, 16)
                        sp.wait_ge(dis_in, 16)

                @block.gpsimd
                def _(pool):
                    for t in super_tiles(pool):
                        wait_alone(pool, edges_in[t.slot], 32 * (t.turn + 1))
                        if not t.first:
                            wait_alone(pool, tile_done[t.slot], t.turn)
                        for k in range(K):
                            pool.indirect_dma_start(
                                out=got[0:t.rows, t.slot, k, :], out_offset=None, in_=node_table,
                                in_offset=bass.IndirectOffsetOnAxis(
                                    ap=src_idx[0:t.rows, t.slot, k:k + 1], axis=0)
                            ).then_inc(gathered[t.slot], 16)

                @block.vector
                def _(dve):
                    if layer == 3:
                        dve.sem_inc(target_used, 1)
                    for t in super_tiles(dve):
                        n, s = t.rows, t.slot
                        first, end, base = window_range(dve, t)
                        wait_alone(dve, edges_in[s], 32 * (t.turn + 1))
                        if layer == 0:
                            nc.vector.tensor_scalar(digit[0:n, 0, :], src_idx[0:n, s, :], 7, None,
                                                    ALU.arith_shift_right)
                            nc.vector.tensor_scalar(digit[0:n, 1, :], src_idx[0:n, s, :], P - 1, None,
                                                    ALU.bitwise_and)
                            if not (t.first and s == 0):
                                wait_alone(dve, counted, t.number)
                            dve.drain()
                            nc.vector.tensor_tensor(
                                hot_hi[0:n], digit[0:n, 0, :].unsqueeze(2).to_broadcast([n, K, HI]),
                                iota_hi[0:n].unsqueeze(1).to_broadcast([n, K, HI]), ALU.is_equal)
                            nc.vector.tensor_tensor(
                                hot_lo[0:n], digit[0:n, 1, :].unsqueeze(2).to_broadcast([n, K, P]),
                                iota_lo[0:n].unsqueeze(1).to_broadcast([n, K, P]), ALU.is_equal)
                            dve.drain().then_inc(digits_made, 1)
                        if layer == 1:
                            dve.wait_ge(attr_in[s], 16 * (t.turn + 1))
                            dve.wait_ge(gathered[s], 16 * K * (t.turn + 1))
                            rows = got[0:n, s, :, :].rearrange("p k f -> p (k f)")
                            nc.vector.tensor_tensor(rows, rows, attr[0:n, s, :], ALU.add).then_inc(added, 1)
                        with dve.Fori(first, end) as j:
                            w = (j - first).with_bounds(min_val=0, max_val=WINDOWS - 1)
                            nc.vector.tensor_scalar(rel[0:n, :], dst_idx[0:n, s, :],
                                                    base_all[0:n, bass.ds(t.number, 1)],
                                                    window_off[0:n, bass.ds(w, 1)],
                                                    ALU.subtract, ALU.subtract)
                            dve.drain()
                            nc.vector.tensor_tensor(
                                pick[0:n], rel[0:n, :].unsqueeze(2).to_broadcast([n, K, W]),
                                iota_w[0:n].unsqueeze(1).to_broadcast([n, K, W]), ALU.is_equal
                            ).then_inc(pick_made, 1)
                            if layer == 3:
                                wait_alone(dve, target_in, 16 * (j + 1))
                                dve.drain()
                                nc.vector.tensor_tensor(share[0:n], pick[0:n],
                                                        target[0:n].unsqueeze(1).to_broadcast([n, K, W]),
                                                        ALU.mult).then_inc(target_used, 1)
                                dve.drain()
                                nc.vector.tensor_reduce(logit[0:n, :], share[0:n], X, ALU.add)
                                wait_alone(dve, gathered[s], 16 * K * (t.turn + 1))
                                dve.drain()
                                nc.vector.tensor_tensor(logit[0:n, :], logit[0:n, :], got[0:n, s, :, D],
                                                        ALU.add).then_inc(logits_made, 1)
                                dve.wait_ge(gated, j + 1)
                                nc.vector.tensor_tensor(msg[0:n], got[0:n, s, :, 0:D],
                                                        gate[0:n, :].unsqueeze(2).to_broadcast([n, K, D]),
                                                        ALU.mult).then_inc(msg_made, 1)
                            dve.wait_ge(summed, j + 1)
                            nodes = agg[:, bass.ds(first_node(base, j), W)]
                            nc.vector.tensor_tensor(nodes, nodes, sums[:, 0:W], ALU.add)
                            dve.drain()
                        dve.drain().then_inc(tile_done[s], 1)
                    if layer == 0:
                        dve.wait_ge(counted, TILES)
                        nc.vector.tensor_copy(degree_lo[:, :], degree[:, 0:HI]).then_inc(degree_copied, 1)
                        dve.wait_ge(degree_turned, 1)
                        nc.vector.tensor_copy(degree_hi[:, :], degree_turned_ps[0:HI, 0:P]).then_inc(turned_copied, 1)
                        dve.wait_ge(dis_in, 16)
                        nc.vector.tensor_scalar(stat[:, :], dis[:, :], 1.0, None, ALU.min)
                        nc.vector.tensor_scalar(dis[:, :], dis[:, :], 1.0, None, ALU.max
                                                ).then_inc(degree_copied, 1)
                        dve.wait_ge(turned_copied, 2)
                        nc.vector.reciprocal(dis[:, :], dis[:, :])
                        dve.drain()
                        nc.vector.tensor_tensor(dis[:, :], dis[:, :], stat[:, :], ALU.mult)

                @block.scalar
                def _(act):
                    if layer == 0:
                        act.wait_ge(degree_copied, 2)
                        nc.scalar.activation(dis[:, :], dis[:, :], ACT.Sqrt).then_inc(turned_copied, 1)
                    if layer == 1:
                        for t in super_tiles(act):
                            act.wait_ge(added, t.number + 1)
                            rows = got[0:t.rows, t.slot, :, :].rearrange("p k f -> p (k f)")
                            nc.scalar.activation(rows, rows, ACT.Relu).then_inc(rectified, 1)
                    if layer == 3:
                        for t in super_tiles(act):
                            first, end, base = window_range(act, t)
                            with act.Fori(first, end) as j:
                                act.wait_ge(logits_made, j + 1)
                                nc.scalar.activation(gate[0:t.rows, :], logit[0:t.rows, :], ACT.Sigmoid
                                                     ).then_inc(gated, 1)

                @block.tensor
                def _(pe):
                    for t in super_tiles(pe):
                        n, s = t.rows, t.slot
                        first, end, base = window_range(pe, t)
                        if layer == 0:
                            pe.wait_ge(digits_made, t.number + 1)
                            for k in range(K):
                                is_first = t.first and s == 0 and k == 0
                                mm = nc.tensor.matmul(degree[:, 0:HI], hot_lo[0:n, k, :], hot_hi[0:n, k, :],
                                                      start=is_first, stop=(n == TAIL and k == K - 1),
                                                      skip_group_check=True)
                            mm.then_inc(counted, 1)
                        if layer in (0, 3):
                            wait_alone(pe, gathered[s], 16 * K * (t.turn + 1))
                        if layer == 1:
                            wait_alone(pe, rectified, t.number + 1)
                        with pe.Fori(first, end) as j:
                            pe.wait_ge(pick_made, j + 1)
                            if layer == 3:
                                pe.wait_ge(msg_made, j + 1)
                            for k in range(K):
                                rows = msg[0:n, k, :] if layer == 3 else got[0:n, s, k, 0:D]
                                mm = nc.tensor.matmul(sums[:, 0:W], rows, pick[0:n, k, :],
                                                      start=(k == 0), stop=(k == K - 1))
                            mm.then_inc(summed, 1)
                    if layer == 0:
                        pe.wait_ge(degree_copied, 1)
                        nc.tensor.transpose(degree_turned_ps[0:HI, 0:P], degree_lo[:, :], ident[:, :]
                                            ).then_inc(degree_turned, 1)

        def sum_by_src():
            with ExitStack() as ph:
                sem = lambda name: ph.enter_context(nc.semaphore(f"{name}2"))
                buf = lambda name, shape, dt=F32: sb(f"{name}2", shape, dt, ph)
                psum = lambda name, shape: ph.enter_context(nc.psum_tensor(f"{name}2", shape, F32))
                src_idx = buf("src_idx", [P, 2, K], I32)
                src_f = buf("src_f", [P, K])
                weight = buf("weight", [P, 2, K])
                src_all = buf("src_all", [P, 2, SUPER], I32)
                dst_all = buf("dst_all", [W, 2, SUPER], I32)
                window_rows = buf("window_rows", [W, D])
                pick = buf("pick", [W, SUPER])
                rows = buf("rows", [P, K * D])
                same = buf("same", [P, K, P])
                junk = buf("junk", [P, K, P], BF16)
                dup = buf("dup", [P, K])
                target = buf("target", [P, 2, K], I32)
                totals = buf("totals", [P, 2, K * D])
                rows_ps = psum("rows_ps", [P, BANK])
                totals_ps = psum("totals_ps", [P, BANK])
                edges_in = [sem(f"edges_in{s}_") for s in (0, 1)]
                tile_done = [sem(f"tile_done{s}_") for s in (0, 1)]
                scattered = [sem(f"scattered{r}_") for r in range(R)]
                window_in, pick_made, expanded, rows_made, totaled, totals_copied = (
                    sem("window_in"), sem("pick_made"), sem("expanded"), sem("rows_made"),
                    sem("totaled"), sem("totals_copied"))
                block = ph.enter_context(nc.Block())

                @block.sync
                def _(sp):
                    for t in super_tiles(sp):
                        if not t.first:
                            sp.wait_ge(tile_done[t.slot], t.turn)
                        n, s = t.rows, t.slot
                        first, end, base = window_range(sp, t)
                        sp.dma_start(src_idx[0:n, s, :], edge_rows(src_rows, t)).then_inc(edges_in[s], 16)
                        sp.dma_start(weight[0:n, s, :], edge_rows(weight_rows, t)).then_inc(edges_in[s], 16)
                        for values, where, parts in ((src, src_all, P), (dst, dst_all, W)):
                            sp.dma_start(where[:, s, 0:n * K],
                                         values.rearrange("(a e) -> a e", a=1)
                                         [:, bass.ds(t.number * SUPER, n * K)].to_broadcast([parts, n * K])
                                         ).then_inc(edges_in[s], 16)
                        with sp.Fori(first, end) as j:
                            sp.wait_ge(expanded, j + 1)
                            sp.dma_start(window_rows[:, :], x2_dram[bass.ds(first_node(base, j), W), :]
                                         ).then_inc(window_in, 16)

                @block.vector
                def _(dve):
                    for t in super_tiles(dve):
                        n, s = t.rows, t.slot
                        first, end, base = window_range(dve, t)
                        dve.wait_ge(edges_in[s], 64 * (t.turn + 1))
                        nc.vector.tensor_copy(src_f[0:n, :], src_idx[0:n, s, :])
                        if not (t.first and s == 0):
                            wait_alone(dve, totaled, t.number)
                        dve.drain()
                        edge = lambda k: src_all[0:n, s, 0:n * K].rearrange("p (r k) -> p k r", k=K)[:, k, :]
                        for k in range(K):
                            nc.vector.tensor_scalar(same[0:n, k, 0:n], edge(k), src_f[0:n, k:k + 1], None,
                                                    ALU.is_equal)
                            nc.vector.scalar_tensor_tensor(
                                out=junk[0:n, k, 0:n], in0=edge(k), scalar=src_f[0:n, k:k + 1],
                                in1=before[0:n, 0:n], op0=ALU.is_equal, op1=ALU.mult,
                                accum_out=dup[0:n, k:k + 1])
                        nc.vector.memset(rows[0:n, :], 0.0)
                        if not t.first:
                            for r in range(R):
                                wait_alone(dve, scattered[r], 16 * (K // R) * (t.number - 1))
                        dve.drain()
                        nc.vector.tensor_scalar(dup[0:n, :], dup[0:n, :], 1.0, None, ALU.min)
                        nc.vector.tensor_scalar(src_f[0:n, :], src_f[0:n, :], -1.0, dump_row[0:n, :],
                                                ALU.mult, ALU.add)
                        dve.drain()
                        nc.vector.tensor_tensor(dup[0:n, :], dup[0:n, :], src_f[0:n, :], ALU.mult)
                        dve.drain()
                        nc.vector.tensor_tensor(target[0:n, s, :], dup[0:n, :], src_idx[0:n, s, :], ALU.add)
                        with dve.Fori(first, end) as j:
                            w = (j - first).with_bounds(min_val=0, max_val=WINDOWS - 1)
                            nc.vector.tensor_scalar(pick[:, 0:n * K], dst_all[:, s, 0:n * K],
                                                    base_all[0:W, bass.ds(t.number, 1)],
                                                    window_node[0:W, bass.ds(w, 1)],
                                                    ALU.subtract, ALU.is_equal).then_inc(pick_made, 1)
                            dve.wait_ge(expanded, j + 2)
                            nc.vector.tensor_tensor(rows[0:n, :], rows[0:n, :], rows_ps[0:n, 0:K * D],
                                                    ALU.add)
                            dve.drain()
                        grid = rows[0:n, :].rearrange("p (k f) -> p k f", k=K)
                        nc.vector.tensor_tensor(grid, grid,
                                                weight[0:n, s, :].unsqueeze(2).to_broadcast([n, K, D]),
                                                ALU.mult).then_inc(rows_made, 1)
                        dve.drain().then_inc(tile_done[s], 1)

                @block.tensor
                def _(pe):
                    pe.sem_inc(expanded, 1)
                    for t in super_tiles(pe):
                        n = t.rows
                        first, end, base = window_range(pe, t)
                        with pe.Fori(first, end) as j:
                            pe.wait_ge(pick_made, j + 1)
                            pe.wait_ge(window_in, 16 * (j + 1))
                            for k in range(K):
                                mm = nc.tensor.matmul(
                                    rows_ps[0:n, k * D:(k + 1) * D],
                                    pick[:, 0:n * K].rearrange("w (r k) -> w k r", k=K)[:, k, :],
                                    window_rows[:, :], start=True, stop=True)
                            mm.then_inc(expanded, 1)
                        pe.wait_ge(rows_made, t.number + 1)
                        if not (t.first and t.slot == 0):
                            pe.wait_ge(totals_copied, t.number)
                        for k in range(K):
                            mm = nc.tensor.matmul(totals_ps[0:n, k * D:(k + 1) * D], same[0:n, k, 0:n],
                                                  rows[0:n, k * D:(k + 1) * D], start=True, stop=True)
                        mm.then_inc(totaled, 1)

                @block.scalar
                def _(act):
                    for t in super_tiles(act):
                        act.wait_ge(totaled, t.number + 1)
                        nc.scalar.copy(totals[0:t.rows, t.slot, :], totals_ps[0:t.rows, 0:K * D]
                                       ).then_inc(totals_copied, 1)

                @block.gpsimd
                def _(pool):
                    for t in super_tiles(pool):
                        n, s = t.rows, t.slot
                        wait_alone(pool, totals_copied, t.number + 1)
                        for k in range(K):
                            r, turn = k % R, k // R
                            if not (t.first and s == 0 and turn == 0):
                                wait_alone(pool, scattered[r], 16 * ((K // R) * t.number + turn))
                            pool.indirect_dma_start(
                                out=z_dram[r],
                                out_offset=bass.IndirectOffsetOnAxis(ap=target[0:n, s, k:k + 1], axis=0),
                                in_=totals[0:n, s, k * D:(k + 1) * D], in_offset=None,
                                compute_op=ALU.add).then_inc(scattered[r], 16)
                    for r in range(R):
                        pool.wait_ge(scattered[r], 16 * (K // R) * TILES)

        def node_phase(layer):
            with ExitStack() as ph:
                sem = lambda name: ph.enter_context(nc.semaphore(f"{name}_n{layer}"))
                buf = lambda name, shape, dt=F32: sb(f"{name}_n{layer}", shape, dt, ph)
                nodes_ps = ph.enter_context(nc.psum_tensor(f"nodes_ps{layer}", [P, 7 * BANK], F32))
                small_ps = ph.enter_context(nc.psum_tensor(f"small_ps{layer}", [P, BANK], F32))
                node_grid = nodes_ps[:, 0:B * D].rearrange("p (b f) -> p b f", f=D)
                turned, centred, rooted, tabled = sem("turned"), sem("centred"), sem("rooted"), sem("tabled")
                ready, stored = sem("ready"), sem("stored")
                inner_turned, inner_copied, hidden, rectified, projected = (
                    sem("inner_turned"), sem("inner_copied"), sem("hidden"), sem("rectified"),
                    sem("projected"))
                params_in, inner_made, parts_in = sem("params_in"), sem("inner_made"), sem("parts_in")
                G = 2
                GROUPS = B // G
                inner = buf("inner", [D, G * P])
                inner2 = buf("inner2", [D, G * P])
                if layer == 1:
                    w1_row, w2_row = buf("w1_row", [D, D]), buf("w2_row", [D, D])
                    wt = buf("wt", [D, 2, D])
                    b1_col, b2_all, scale = buf("b1_col", [D, 1]), buf("b2_all", [P, D]), buf("scale", [P, 1])
                    PARAMS = 5
                if layer == 2:
                    wt = buf("wt", [D, 2, D])
                    parts = buf("parts", [P, B * D])
                    PARAMS = 1
                if layer == 2:
                    y = buf("y", [P, B, YC])
                    vec_src, vec_tgt, bias = buf("vec_src", [P, D]), buf("vec_tgt", [P, D]), buf("bias", [P, 1])
                    target = buf("target", [P, B])
                    PARAMS += 3
                assert B % G == 0
                block = ph.enter_context(nc.Block())
                last_layer = L - 1

                @block.sync
                def _(sp):
                    row = lambda v: v.rearrange("(a n) -> a n", a=1)
                    if layer == 1:
                        sp.dma_start(w1_row[:, :], w1[last_layer, :, :]).then_inc(params_in, 16)
                        sp.dma_start(w2_row[:, :], w2[last_layer, :, :]).then_inc(params_in, 16)
                        sp.dma_start(b1_col[:, :], b1[last_layer, :].rearrange("(n a) -> n a", a=1)
                                     ).then_inc(params_in, 16)
                        sp.dma_start(b2_all[:, :], b2[last_layer:last_layer + 1, :].to_broadcast([P, D])
                                     ).then_inc(params_in, 16)
                        sp.dma_start(scale[:, :], row(eps)[:, last_layer:last_layer + 1].to_broadcast([P, 1])
                                     ).then_inc(params_in, 16)
                    if layer == 2:
                        sp.dma_start(wt[:, 0, :], w_lin).then_inc(params_in, 16)
                        sp.dma_start(vec_src[:, :], row(w_src).to_broadcast([P, D])).then_inc(params_in, 16)
                        sp.dma_start(vec_tgt[:, :], row(w_tgt).to_broadcast([P, D])).then_inc(params_in, 16)
                        sp.dma_start(bias[:, :], row(gate_bias).to_broadcast([P, 1])).then_inc(params_in, 16)
                        sp.dma_start(hs[:, :, :].rearrange("p b f -> p (b f)"), node_rows(z_dram[0])
                                     ).then_inc(parts_in, 16)
                        for r in range(1, R):
                            if r > 1:
                                sp.wait_ge(inner_made, r - 1)
                            sp.dma_start(parts[:, :], node_rows(z_dram[r])).then_inc(parts_in, 16)
                    sp.wait_ge(ready, 1)
                    flat = xs[:, :, :].rearrange("p b f -> p (b f)")
                    if layer < 2:
                        sp.dma_start(node_rows((x1_dram, x2_dram)[layer]), flat).then_inc(stored, 16)
                        sp.wait_ge(stored, 16)
                    if layer == 2:
                        sp.dma_start(node_rows(y_dram), y[:, :, :].rearrange("p b f -> p (b f)")
                                     ).then_inc(stored, 16)
                        sp.dma_start(b_dram[0:NP, :].rearrange("(p b) q -> p (b q)", b=B), target[:, :]
                                     ).then_inc(stored, 16)
                        sp.wait_ge(stored, 32)
                    if layer == 3:
                        sp.dma_start(out[0:(P - 1) * B, :].rearrange("(p b) f -> p (b f)", b=B),
                                     flat[0:P - 1, :]).then_inc(stored, 16)
                        sp.dma_start(out[(P - 1) * B:N, :].rearrange("(p b) f -> p (b f)", b=LASTROWS),
                                     flat[P - 1:P, 0:LASTROWS * D]).then_inc(stored, 16)
                        sp.wait_ge(stored, 32)

                @block.tensor
                def _(pe):
                    if layer == 1:
                        pe.wait_ge(params_in, 16 * PARAMS)
                        nc.tensor.transpose(small_ps[0:D, 0:D], w1_row[:, :], ident[0:D, 0:D])
                        nc.tensor.transpose(small_ps[0:D, D:2 * D], w2_row[:, :], ident[0:D, 0:D]
                                            ).then_inc(tabled, 1)
                    if layer != 2:
                        by_block = agg[:, 0:NP].rearrange("f (p b) -> f b p", b=B)
                        for b in range(B):
                            mm = nc.tensor.transpose(node_grid[:, b, :], by_block[:, b, :], ident[0:D, 0:D])
                        mm.then_inc(turned, 1)
                    if layer in (1, 2):
                        pe.wait_ge(inner_made, 1 if layer == 1 else R - 1)
                        if layer == 1:
                            pe.wait_ge(tabled, 2)
                        for g in range(GROUPS):
                            for q in range(G):
                                mm = nc.tensor.transpose(small_ps[0:D, q * P:(q + 1) * P],
                                                         hs[:, g * G + q, :], ident[:, :])
                            mm.then_inc(inner_turned, 1)
                            pe.wait_ge(inner_copied, g + 1)
                            last = inner
                            if layer == 1:
                                nc.tensor.matmul(small_ps[0:D, G * P:2 * G * P], wt[:, 0, :], inner[:, :],
                                                 start=True, stop=True).then_inc(hidden, 1)
                                pe.wait_ge(rectified, g + 1)
                                last = inner2
                            for q in range(G):
                                mm = nc.tensor.matmul(node_grid[:, g * G + q, :], last[:, q * P:(q + 1) * P],
                                                      wt[:, 1 if layer == 1 else 0, :], start=True, stop=True)
                        mm.then_inc(projected, 1)

                @block.scalar
                def _(act):
                    if layer in (1, 2):
                        for g in range(GROUPS):
                            act.wait_ge(inner_turned, g + 1)
                            nc.scalar.copy(inner[:, :], small_ps[0:D, 0:G * P]).then_inc(inner_copied, 1)
                            if layer == 1:
                                act.wait_ge(hidden, g + 1)
                                nc.scalar.activation(inner2[:, :], small_ps[0:D, G * P:2 * G * P], ACT.Relu,
                                                     bias=b1_col[:, :]).then_inc(rectified, 1)
                    act.wait_ge(centred, 1)
                    nc.scalar.activation(stat[:, :], stat[:, :], ACT.Sqrt, bias=eps_col[:, :], scale=1.0 / D
                                         ).then_inc(rooted, 1)

                @block.vector
                def _(dve):
                    across = lambda v: v.unsqueeze(2).to_broadcast([P, B, D])
                    along = lambda v: v.unsqueeze(1).to_broadcast([P, B, D])
                    if layer == 1:
                        dve.wait_ge(tabled, 1)
                        nc.vector.tensor_copy(wt[:, :, :].rearrange("f a g -> f (a g)"),
                                              small_ps[0:D, 0:2 * D]).then_inc(tabled, 1)
                        nc.vector.tensor_scalar(scale[:, :], scale[:, :], 1.0, None, ALU.add)
                        dve.wait_ge(turned, 1)
                        dve.drain()
                        nc.vector.scalar_tensor_tensor(
                            out=hs[:, :, :], in0=xs[:, :, :], scalar=scale[:, :],
                            in1=node_grid, op0=ALU.mult, op1=ALU.add)
                        dve.drain().then_inc(inner_made, 1)
                        nc.vector.memset(agg[:, :], 0.0)
                        dve.wait_ge(projected, 1)
                        nc.vector.tensor_tensor(hs[:, :, :], along(b2_all[:, :]), node_grid, ALU.add)
                        dve.drain()
                        nc.vector.tensor_scalar(hs[:, :, :], hs[:, :, :], 0.0, None, ALU.max)
                        dve.drain()
                        nc.vector.tensor_tensor(xs[:, :, :], xs[:, :, :], hs[:, :, :], ALU.add)
                    if layer == 2:
                        flat = hs[:, :, :].rearrange("p b f -> p (b f)")
                        for r in range(1, R):
                            dve.wait_ge(parts_in, 16 * (r + 1))
                            nc.vector.tensor_tensor(flat, flat, parts[:, :], ALU.add)
                            dve.drain().then_inc(inner_made, 1)
                        dve.wait_ge(projected, 1)
                    if layer == 3:
                        dve.wait_ge(turned, 1)
                        nc.vector.tensor_tensor(hs[:, :, :], across(dis[:, :]), node_grid, ALU.mult)
                        dve.drain()
                        nc.vector.tensor_tensor(xs[:, :, :], xs[:, :, :], hs[:, :, :], ALU.add)
                    if layer in (0, 2):
                        if layer == 0:
                            dve.wait_ge(turned, 1)
                        nc.vector.tensor_tensor(xs[:, :, :], xs[:, :, :], node_grid, ALU.add)
                    dve.drain()
                    if layer == 0:
                        nc.vector.memset(agg[:, :], 0.0)
                    nc.vector.tensor_reduce(stat[:, :], xs[:, :, :], X, ALU.add)
                    dve.drain()
                    nc.vector.tensor_scalar(stat[:, :], stat[:, :], 1.0 / D, None, ALU.mult)
                    dve.drain()
                    nc.vector.tensor_tensor(xs[:, :, :], xs[:, :, :], across(stat[:, :]), ALU.subtract)
                    dve.drain()
                    nc.vector.tensor_tensor(tmp[:, :, :], xs[:, :, :], xs[:, :, :], ALU.mult)
                    dve.drain()
                    nc.vector.tensor_reduce(stat[:, :], tmp[:, :, :], X, ALU.add).then_inc(centred, 1)
                    dve.wait_ge(rooted, 1)
                    nc.vector.reciprocal(stat[:, :], stat[:, :])
                    dve.drain()
                    nc.vector.tensor_tensor(xs[:, :, :], xs[:, :, :], across(stat[:, :]), ALU.mult)
                    dve.drain()
                    if layer == 2:
                        dve.wait_ge(params_in, 16 * PARAMS)
                        nc.vector.memset(y[:, :, D:YC], 0.0)
                        nc.vector.tensor_tensor(y[:, :, 0:D], xs[:, :, :], across(dis[:, :]), ALU.mult)
                        nc.vector.tensor_tensor(tmp[:, :, :], xs[:, :, :], along(vec_src[:, :]), ALU.mult)
                        nc.vector.tensor_tensor(hs[:, :, :], xs[:, :, :], along(vec_tgt[:, :]), ALU.mult)
                        dve.drain()
                        nc.vector.tensor_reduce(y[:, :, D], tmp[:, :, :], X, ALU.add)
                        nc.vector.tensor_reduce(target[:, :], hs[:, :, :], X, ALU.add)
                        dve.drain()
                        nc.vector.tensor_scalar(target[:, :], target[:, :], bias[:, :], None, ALU.add)
                    dve.drain().then_inc(ready, 1)

        sum_by_dst(0)
        node_phase(0)
        sum_by_dst(1)
        node_phase(1)
        sum_by_src()
        node_phase(2)
        sum_by_dst(3)
        node_phase(3)


_INS = ["x", "src", "dst", "edge_attr_32", "edge_weight", "L1_gnn_eps", "L1_gnn_W1", "L1_gnn_b1",
        "L1_gnn_W2", "L1_gnn_b2", "L2_gnn_weight", "L3_gnn_w_src", "L3_gnn_w_tgt", "L3_gnn_gate_bias"]


def kernel(**inputs):
    import numpy as np
    import concourse.bacc as bacc
    from concourse.bass_utils import run_bass_kernel_spmd

    nc = bacc.Bacc("TRN2", target_bir_lowering=False, num_devices=1)
    arrays, args = {}, []
    for name in _INS:
        a = np.ascontiguousarray(inputs[name])
        arrays[name] = a
        args.append(nc.dram_tensor(name, a.shape, mybir.dt.from_np(a.dtype), kind="ExternalInput").ap())
    n, d = inputs["x"].shape
    args.append(nc.dram_tensor("out", (n, d), F32, kind="ExternalOutput").ap())
    build_program(nc, *args)
    result = run_bass_kernel_spmd(nc, [arrays], core_ids=[0])
    return result.results[0]["out"]
```

```python
from contextlib import ExitStack

import concourse.bass as bass
from concourse import mybir

F32 = mybir.dt.float32
BF16 = mybir.dt.bfloat16
F16 = mybir.dt.float16
I32 = mybir.dt.int32
ALU = mybir.AluOpType
ACT = mybir.ActivationFunctionType
X = mybir.AxisListType.X

P = 128
K = 12
SUPER = K * P
W = 64
LOG_W = 6
C = 7
CD = K * C
ONE_HOTS = 4
R = 4
BANK = 512
EPS = 1e-5


class Tile:

    def __init__(self, number, turn, slot, rows, first):
        self.number, self.turn, self.slot, self.rows, self.first = number, turn, slot, rows, first


def build_program(nc, x, src, dst, edge_attr, edge_weight, eps, w1, b1, w2, b2, w_lin, w_src, w_tgt,
                  gate_bias, out):
    N, D = x.shape
    E = src.shape[0]
    L = eps.shape[0]
    B = -(-N // P)
    NP = P * B
    NT = -(-max(NP + W, N + P) // P) * P
    FULL = E // SUPER
    TAIL = (E - FULL * SUPER) // K
    TILES = FULL + 1
    PAIRS = FULL // 2
    assert FULL % 2 == 0 and E == FULL * SUPER + TAIL * K and 0 < TAIL < P and D == 32
    WINDOWS = -(-N // W) + 1
    MOST = TILES * WINDOWS
    CHUNKS = -(-TILES // P)
    HI = -(-N // P)
    DR = D + 1
    YC = 36
    HALF = HI // 2
    assert HI % 2 == 0 and HALF * C <= BANK and CD <= P and FULL % 4 == 0
    LASTROWS = N - (P - 1) * B

    def node_rows(table, cols=D):
        return table[0:NP, :].rearrange("(p b) f -> p (b f)", b=B)

    src_rows = src.rearrange("(r k) -> r k", k=K)
    dst_rows = dst.rearrange("(r k) -> r k", k=K)
    weight_rows = edge_weight.rearrange("(r k) -> r k", k=K)
    attr_rows = edge_attr.rearrange("(r k) f -> r (k f)", k=K)

    x1_dram = nc.dram_tensor("x1_table", (NT, D), F32, kind="Internal").ap()
    x2_dram = nc.dram_tensor("x2_table", (NT, D), F32, kind="Internal").ap()
    y_dram = nc.dram_tensor("y_table", (NT, YC), F32, kind="Internal").ap()
    z_dram = [nc.dram_tensor(f"z_part{r}", (NT, D), F32, kind="Internal").ap() for r in range(R)]
    b_dram = nc.dram_tensor("target_logit", (NT, 1), F32, kind="Internal").ap()
    deg_dram = nc.dram_tensor("degree", (HI, P), F32, kind="Internal").ap()
    win_dram = nc.dram_tensor("window_table", (CHUNKS * P, 4), I32, kind="Internal").ap()
    base_dram = nc.dram_tensor("window_base", (CHUNKS * P, 1), F32, kind="Internal").ap()

    with ExitStack() as ctx:
        def sb(name, shape, dt=F32, scope=ctx):
            return scope.enter_context(nc.sbuf_tensor(name, shape, dt))

        iota_w = sb("iota_w", [P, W])
        iota_hi = sb("iota_hi", [P, HI])
        iota_lo = sb("iota_lo", [P, P])
        window_off = sb("window_off", [P, WINDOWS])
        window_node = sb("window_node", [P, WINDOWS])
        dump_row = sb("dump_row", [P, 1])
        ident = sb("ident", [P, P])
        rank_bits = sb("rank_bits", [P, 1], I32)
        rank = sb("rank", [P, 2])
        below = sb("below", [P, P])
        ones = sb("ones", [P, P])
        eps_col = sb("eps_col", [P, 1])
        windows = sb("windows", [1, TILES * 4], I32)
        base_all = sb("base_all", [P, TILES])
        iota_pair = sb("iota_pair", [P, HI * C], F16)
        group_low = sb("group_low", [K, CHUNKS * P])
        pair_node = sb("pair_node", [CD, TILES])
        xs = sb("xs", [P, B, D])
        hs = sb("hs", [P, B, D])
        tmp = sb("tmp", [P, B, D])
        agg = sb("agg", [D, NP + W])
        stat = sb("stat", [P, B])
        dis = sb("dis", [P, B])

        def super_tiles(eng):
            for slot in (0, 1):
                yield Tile(slot, 0, slot, P, True)
            with eng.Fori(1, PAIRS) as i:
                for slot in (0, 1):
                    yield Tile(2 * i + slot, i, slot, P, False)
            yield Tile(2 * PAIRS, PAIRS, 0, TAIL, False)

        def window_range(eng, tile, with_base=True):
            entry = lambda q, low, high: eng.value_load(windows[0:1, bass.ds(4 * tile.number + q, 1)],
                                                        min_val=low, max_val=high)
            first, end = entry(0, 0, MOST), entry(1, 1, MOST)
            return (first, end, entry(2, -W * MOST, N)) if with_base else (first, end)

        passed = ctx.enter_context(nc.semaphore("passed"))

        def wait_alone(eng, semaphore, value):
            eng.wait_ge(semaphore, value)
            eng.sem_inc(passed, 1)

        def first_node(base, j):
            return (base + W * j).with_bounds(min_val=0, max_val=NP)

        def edge_rows(rows, tile):
            return rows[bass.ds(tile.number * P, tile.rows), :]

        with ExitStack() as ph:
            sem = lambda name: ph.enter_context(nc.semaphore(name))
            dst_tiles = sb("dst_tiles", [P, CHUNKS, SUPER], I32, ph)
            low = sb("low", [P, CHUNKS], F32, ph)
            high = sb("high", [P, CHUNKS], F32, ph)
            span = sb("span", [P, CHUNKS], I32, ph)
            count = sb("count", [P, CHUNKS], F32, ph)
            start = sb("start", [P, CHUNKS], F32, ph)
            table = sb("table", [P, CHUNKS, 4], I32, ph)
            group_min = sb("group_min", [P, CHUNKS, K], F32, ph)
            group_max = sb("group_max", [P, CHUNKS, K], F32, ph)
            worst = sb("worst", [P, 2], F32, ph)
            repeat = sb("repeat", [K, CD], F32, ph)
            number = sb("number", [P, 1], F32, ph)
            offset = sb("offset", [CD, 1], F32, ph)
            prefix = ph.enter_context(nc.psum_tensor("prefix", [P, 3, 4], F32))
            low_ps = ph.enter_context(nc.psum_tensor("low_ps", [K, BANK], F32))
            pair_ps = ph.enter_context(nc.psum_tensor("pair_ps", [CD, BANK], F32))
            turned, low_copied, repeated = sem("turned"), sem("low_copied"), sem("repeated")
            numbered = sem("numbered")
            dst_in, x_in, filled, made, spans, prefixed, table_made = (
                sem("dst_in"), sem("x_in"), sem("filled"), sem("made"), sem("spans"), sem("prefixed"),
                sem("table_made"))
            table_out, windows_in, zeroed, cleared = (
                sem("table_out"), sem("windows_in"), sem("zeroed"), sem("cleared"))
            last = TILES - 1 - (CHUNKS - 1) * P
            block = ph.enter_context(nc.Block())

            @block.sync
            def _(sp):
                for c in range(CHUNKS - 1):
                    sp.dma_start(dst_tiles[:, c, :],
                                 dst[c * P * SUPER:(c + 1) * P * SUPER]
                                 .rearrange("(t e) -> t e", e=SUPER)).then_inc(dst_in, 16)
                sp.dma_start(dst_tiles[0:last, CHUNKS - 1, :],
                             dst[(CHUNKS - 1) * P * SUPER:FULL * SUPER]
                             .rearrange("(t e) -> t e", e=SUPER)).then_inc(dst_in, 16)
                sp.dma_start(dst_tiles[last:last + 1, CHUNKS - 1, :],
                             dst[E - SUPER:E].rearrange("(t e) -> t e", e=SUPER)).then_inc(dst_in, 16)
                sp.wait_ge(filled, 2)
                sp.dma_start(xs[0:P - 1, :, :].rearrange("p b f -> p (b f)"),
                             x[0:(P - 1) * B, :].rearrange("(p b) f -> p (b f)", b=B)).then_inc(x_in, 16)
                sp.dma_start(xs[P - 1:P, 0:LASTROWS, :].rearrange("p b f -> p (b f)"),
                             x[(P - 1) * B:N, :].rearrange("(p b) f -> p (b f)", b=LASTROWS)
                             ).then_inc(x_in, 16)
                sp.dma_start(tmp[:, 0:N // P, :], x[0:N // P * P, :].rearrange("(h l) f -> l h f", l=P)
                             ).then_inc(x_in, 16)
                sp.dma_start(tmp[0:N - N // P * P, HI - 1, :], x[N // P * P:N, :]).then_inc(x_in, 16)
                sp.wait_ge(cleared, 1)
                for r in range(R):
                    sp.dma_start(node_rows(z_dram[r]), hs[:, :, :].rearrange("p b f -> p (b f)")
                                 ).then_inc(zeroed, 16)
                    sp.dma_start(z_dram[r][NP:NT, :], hs[0:NT - NP, 0, :]).then_inc(zeroed, 16)
                sp.dma_start(x2_dram[NP:NT, :], hs[0:NT - NP, 0, :]).then_inc(zeroed, 16)
                sp.dma_start(b_dram[NP:NT, :], hs[0:NT - NP, 0, 0:1]).then_inc(zeroed, 16)
                sp.wait_ge(table_made, 2)
                sp.dma_start(win_dram.rearrange("(c p) q -> p c q", p=P), table[:, :, :]
                             ).then_inc(table_out, 16)
                with nc.allow_non_contiguous_dma(reason="one word per tile"):
                    sp.dma_start(base_dram.rearrange("(c p) q -> p (c q)", p=P), low[:, :]
                                 ).then_inc(table_out, 16)
                sp.wait_ge(table_out, 32)
                sp.dma_start(windows[:, :], win_dram[0:TILES, :].rearrange("t q -> (t q)")
                             .rearrange("(a n) -> a n", a=1)).then_inc(windows_in, 16)
                sp.dma_start(base_all[:, :], base_dram[0:TILES, :].rearrange("t q -> q t")
                             .to_broadcast([P, TILES])).then_inc(windows_in, 16)
                sp.wait_ge(windows_in, 32)
                sp.wait_ge(zeroed, 16 * (2 * R + 2))
                sp.wait_ge(x_in, 64)

            @block.gpsimd
            def _(pool):
                pool.memset(xs[:, :, :], 0.0).then_inc(filled, 1)
                pool.memset(tmp[:, :, :], 0.0).then_inc(filled, 1)
                pool.memset(ident[:, :], 0.0).then_inc(made, 1)
                pool.memset(ones[:, :], 1.0).then_inc(made, 1)
                pool.wait_ge(made, 2)
                pool.affine_select(out=ident[:, :], in_=ident[:, :], compare_op=ALU.not_equal, fill=1.0,
                                   base=0, pattern=[[-1, P]], channel_multiplier=1)
                pool.affine_select(out=below[:, :], in_=ones[:, :], compare_op=ALU.is_gt, fill=0.0,
                                   base=0, pattern=[[1, P]], channel_multiplier=-1).then_inc(made, 1)
                pool.affine_select(out=repeat[:, :], in_=ones[0:K, 0:CD], compare_op=ALU.is_ge, fill=0.0,
                                   base=0, pattern=[[1, CD]], channel_multiplier=-C).then_inc(made, 1)
                pool.wait_ge(made, 4)
                pool.affine_select(out=repeat[:, :], in_=repeat[:, :], compare_op=ALU.is_ge, fill=0.0,
                                   base=C - 1, pattern=[[-1, CD]], channel_multiplier=C).then_inc(made, 1)
                for tile, step, num, base, mult in ((iota_w, 1, W, 0, 0), (iota_hi, 1, HI, 0, 0),
                                                    (iota_lo, 1, P, 0, 0), (window_off, W, WINDOWS, 0, 0),
                                                    (rank_bits, 0, 1, 190 << 23, -(1 << 23)),
                                                    (iota_pair, 1, HI * C, 0, 0), (number, 0, 1, 0, 1),
                                                    (window_node, W, WINDOWS, 0, 1), (dump_row, 1, 1, N, 1)):
                    pool.iota(tile[:, :], pattern=[[step, num]], base=base, channel_multiplier=mult,
                              allow_small_or_imprecise_dtypes=True).then_inc(numbered, 1)

            @block.vector
            def _(dve):
                nc.vector.memset(hs[:, :, :], 0.0).then_inc(cleared, 1)
                nc.vector.memset(agg[:, :], 0.0)
                nc.vector.memset(eps_col[:, :], EPS)
                nc.vector.memset(low[:, :], 0.0)
                nc.vector.memset(high[:, :], 0.0)
                nc.vector.memset(group_min[:, :, :], 0.0)
                nc.vector.memset(group_max[:, :, :], 0.0)
                nc.vector.memset(table[:, :, :], 0)
                dve.wait_ge(dst_in, 16 * (CHUNKS + 1))
                dve.drain()
                for c in range(CHUNKS):
                    rows = P if c < CHUNKS - 1 else last + 1
                    nc.vector.tensor_reduce(low[0:rows, c:c + 1], dst_tiles[0:rows, c, :], X, ALU.min)
                    nc.vector.tensor_reduce(high[0:rows, c:c + 1], dst_tiles[0:rows, c, :], X, ALU.max)
                    groups = dst_tiles[0:rows, c, :].rearrange("p (k e) -> p k e", k=K)
                    nc.vector.tensor_reduce(group_min[0:rows, c, :], groups, X, ALU.min)
                    nc.vector.tensor_reduce(group_max[0:rows, c, :], groups, X, ALU.max)
                dve.drain()
                nc.vector.tensor_tensor(span[:, :], high[:, :], low[:, :], ALU.subtract)
                dve.drain()
                nc.vector.tensor_scalar(span[:, :], span[:, :], LOG_W, None, ALU.arith_shift_right)
                dve.drain()
                nc.vector.tensor_scalar(count[:, :], span[:, :], 1.0, None, ALU.add)
                nc.vector.tensor_tensor(group_max[:, :, :], group_max[:, :, :], group_min[:, :, :],
                                        ALU.subtract)
                dve.drain()
                nc.vector.tensor_reduce(worst[:, 0:1], group_max[:, :, :].rearrange("p c k -> p (c k)"), X,
                                        ALU.max)
                nc.vector.tensor_reduce(worst[:, 1:2], count[:, :], X, ALU.max)
                dve.drain()
                nc.vector.tensor_scalar(worst[:, 0:1], worst[:, 0:1], float(C), None, ALU.is_ge)
                nc.vector.tensor_scalar(worst[:, 1:2], worst[:, 1:2], 1.0, None, ALU.is_gt)
                dve.drain()
                nc.vector.tensor_tensor(worst[:, 0:1], worst[:, 0:1], worst[:, 1:2], ALU.add)
                dve.drain().then_inc(spans, 1)
                dve.wait_ge(prefixed, 1)
                nc.vector.tensor_copy(start[:, :], prefix[:, 0, 0:CHUNKS])
                for c in range(CHUNKS):
                    nc.vector.tensor_scalar(table[:, c, 3:4], prefix[:, 2, 0:1], 1.0, None, ALU.min)
                for c in range(CHUNKS - 1):
                    for later in range(c + 1, CHUNKS):
                        dve.drain()
                        nc.vector.tensor_tensor(start[:, later:later + 1], start[:, later:later + 1],
                                                prefix[:, 1, c:c + 1], ALU.add)
                dve.drain()
                nc.vector.tensor_copy(table[:, :, 0], start[:, :])
                nc.vector.tensor_tensor(table[:, :, 1], start[:, :], count[:, :], ALU.add)
                dve.drain()
                nc.vector.tensor_scalar(count[:, :], start[:, :], -float(W), None, ALU.mult)
                dve.drain()
                nc.vector.tensor_tensor(table[:, :, 2], count[:, :], low[:, :], ALU.add)
                dve.drain().then_inc(table_made, 2)
                dve.wait_ge(numbered, 9)
                nc.vector.tensor_copy(rank[:, 0:1], rank_bits[:, :].bitcast(F32))
                nc.vector.tensor_scalar(rank[:, 1:2], rank_bits[:, :].bitcast(F32), 2.5, None, ALU.mult)
                dve.wait_ge(turned, 1)
                nc.vector.tensor_copy(group_low[:, :], low_ps[:, 0:CHUNKS * P]).then_inc(low_copied, 1)
                dve.wait_ge(repeated, 1)
                dve.wait_ge(windows_in, 32)
                nc.vector.tensor_scalar(offset[:, :], pair_ps[:, BANK - 1:BANK], -float(C), number[0:CD, :],
                                        ALU.mult, ALU.add)
                nc.vector.tensor_tensor(pair_node[:, :], pair_ps[:, 0:TILES], base_all[0:CD, :], ALU.subtract)
                dve.drain()
                nc.vector.tensor_scalar(pair_node[:, :], pair_node[:, :], offset[:, :], None, ALU.add)

            @block.tensor
            def _(pe):
                pe.wait_ge(spans, 1)
                pe.wait_ge(made, 5)
                nc.tensor.matmul(prefix[:, 0, 0:CHUNKS], below[:, :], count[:, :], start=True, stop=True)
                nc.tensor.matmul(prefix[:, 2, 0:1], ones[:, :], worst[:, 0:1], start=True, stop=True)
                nc.tensor.matmul(prefix[:, 1, 0:CHUNKS], ones[:, :], count[:, :], start=True, stop=True
                                 ).then_inc(prefixed, 1)
                for c in range(CHUNKS):
                    mm = nc.tensor.transpose(low_ps[:, c * P:(c + 1) * P], group_min[:, c, :], ident[:, :])
                mm.then_inc(turned, 1)
                pe.wait_ge(low_copied, 1)
                pe.wait_ge(numbered, 9)
                nc.tensor.matmul(pair_ps[:, 0:CHUNKS * P], repeat[:, :], group_low[:, :], start=True, stop=True)
                nc.tensor.matmul(pair_ps[:, BANK - 1:BANK], repeat[:, :], number[0:K, :], start=True, stop=True
                                 ).then_inc(repeated, 1)

        class Pair:

            def __init__(self, turn, slot, first=False, last=False):
                self.turn, self.slot, self.first, self.last = turn, slot, first, last
                self.number = 2 * turn + slot
                self.gather = Tile(2 * self.number, turn, slot, P, first)
                self.counted = 2 * self.number + 1
                self.start = first and slot == 0

            def next(self):
                return Pair(self.turn + self.slot, 1 - self.slot)

            def previous(self):
                return Pair(self.turn - (1 - self.slot), 1 - self.slot)

        TURNS = PAIRS // 2

        def pairs(eng):
            for slot in (0, 1):
                yield Pair(0, slot, first=True)
            with eng.Fori(1, TURNS - 1) as i:
                for slot in (0, 1):
                    yield Pair(i, slot)
            for slot in (0, 1):
                yield Pair(TURNS - 1, slot, last=(slot == 1))

        LAST_PAIR = Pair(TURNS - 1, 1)
        TAIL_TILE = Tile(2 * PAIRS, TURNS, 0, TAIL, False)

        def sum_by_dst(layer):
            cols = YC if layer == 3 else D
            node_table = {0: x, 1: x1_dram[0:NP, :], 3: y_dram[0:NP, :]}[layer]
            with ExitStack() as ph:
                sem = lambda name: ph.enter_context(nc.semaphore(f"{name}{layer}"))
                buf = lambda name, shape, dt=F32: sb(f"{name}{layer}", shape, dt, ph)
                psum = lambda name, shape: ph.enter_context(nc.psum_tensor(f"{name}{layer}", shape, F32))
                src_idx = buf("src_idx", [P, 2, K], I32)
                dst_idx = buf("dst_idx", [P, 2, K], I32)
                got = buf("got", [P, 2, K, cols])
                rel = buf("rel", [P, K])
                pick = buf("pick", [P, K, W])
                sums = psum("sums", [D, BANK])
                edges_in = [sem(f"edges_in{s}_") for s in (0, 1)]
                gathered = [sem(f"gathered{s}_") for s in (0, 1)]
                tile_done = [sem(f"tile_done{s}_") for s in (0, 1)]
                pick_made, summed = sem("pick_made"), sem("summed")
                if layer == 0:
                    parts = buf("parts", [P, HI, 3, D], BF16)
                    edge_group = buf("edge_group", [K, 2, 2, P], I32)
                    digit = buf("digit", [K, 2, P], I32)
                    span_node = buf("span_node", [K, P])
                    label = buf("label", [K, 2, 2, P])
                    column = buf("column", [P, 2, 2 * K])
                    hot_pair = buf("hot_pair", [P, ONE_HOTS, HI * C], BF16)
                    hot_low = buf("hot_low", [P, 2, K, P], BF16)
                    counts = [buf(f"counts{q}_", [P, HI, CD], BF16) for q in (0, 1)]
                    pair_rows = buf("pair_rows", [CD, 3 * D])
                    pair_pick = buf("pair_pick", [CD, W])
                    label_ps = psum("label_ps", [P, BANK])
                    counts_ps = psum("counts_ps", [P, 4 * BANK])
                    pair_ps = psum("pair_ps", [CD, BANK])
                    pair_sums = psum("pair_sums", [D, BANK])
                    groups_in = [sem(f"groups_in{q}_") for q in (0, 1)]
                    labeled, label_turned, one_hots, group_counted, counts_copied = (
                        sem("labeled"), sem("label_turned"), sem("one_hots"), sem("group_counted"),
                        sem("counts_copied"))
                    multiplied, pair_rows_made, pairs_summed = (
                        sem("multiplied"), sem("pair_rows_made"), sem("pairs_summed"))

                def regular_or_not(eng, regular, general):
                    if layer != 0:
                        general()
                        return
                    irregular = eng.value_load(windows[0:1, 3:4], min_val=0, max_val=1)
                    with eng.If(irregular < 1):
                        regular()
                    if general:
                        with eng.Else():
                            general()

                if layer == 1:
                    digit = buf("digit", [P, 2, K], I32)
                    hot_hi = buf("hot_hi", [P, K, HI], BF16)
                    hot_lo = buf("hot_lo", [P, K, P], BF16)
                    degree = psum("degree_ps", [P, BANK])
                    degree_turned_ps = psum("degree_turned_ps", [P, BANK])
                    digits_made, counted, degree_copied, degree_turned, turned_copied, degree_out, dis_in = (
                        sem("digits_made"), sem("counted"), sem("degree_copied"), sem("degree_turned"),
                        sem("turned_copied"), sem("degree_out"), sem("dis_in"))
                    degree_lo = buf("degree_lo", [P, HI])
                    degree_hi = buf("degree_hi", [HI, P])
                    attr = buf("attr", [P, 2, K * D])
                    attr_in = [sem(f"attr_in{s}_") for s in (0, 1)]
                    added, rectified = sem("added"), sem("rectified")
                if layer == 3:
                    target = buf("target", [P, W])
                    share = buf("share", [P, K, W])
                    logit = buf("logit", [P, K])
                    gate = buf("gate", [P, K])
                    msg = buf("msg", [P, K, D])
                    target_in, target_used, logits_made, gated, msg_made = (
                        sem("target_in"), sem("target_used"), sem("logits_made"), sem("gated"),
                        sem("msg_made"))
                block = ph.enter_context(nc.Block())

                @block.sync
                def _(sp):
                    def load(t):
                        if not t.first:
                            sp.wait_ge(tile_done[t.slot], t.turn)
                        sp.dma_start(src_idx[0:t.rows, t.slot, :], edge_rows(src_rows, t)
                                     ).then_inc(edges_in[t.slot], 16)
                        sp.dma_start(dst_idx[0:t.rows, t.slot, :], edge_rows(dst_rows, t)
                                     ).then_inc(edges_in[t.slot], 16)

                    def regular():
                        for p in pairs(sp):
                            load(p.gather)
                            if not p.first:
                                sp.wait_ge(labeled, p.number - 1)
                            for q, values in enumerate((src, dst)):
                                sp.dma_start(edge_group[:, p.slot, q, :],
                                             values[0:FULL * SUPER].rearrange("(g e) -> g e", e=P)
                                             [bass.ds(p.counted * K, K), :]).then_inc(groups_in[p.slot], 16)
                        load(TAIL_TILE)

                    def general():
                        for t in super_tiles(sp):
                            load(t)
                            if layer == 1:
                                sp.dma_start(attr[0:t.rows, t.slot, :], edge_rows(attr_rows, t)
                                             ).then_inc(attr_in[t.slot], 16)
                            if layer == 3:
                                first, end, base = window_range(sp, t)
                                with sp.Fori(first, end) as j:
                                    sp.wait_ge(target_used, j + 1)
                                    sp.dma_start(target[:, :], b_dram[bass.ds(first_node(base, j), W), :]
                                                 .rearrange("n q -> q n").to_broadcast([P, W])
                                                 ).then_inc(target_in, 16)

                    regular_or_not(sp, regular, general)
                    if layer == 1:
                        sp.wait_ge(turned_copied, 1)
                        sp.dma_start(deg_dram, degree_hi[:, :]).then_inc(degree_out, 16)
                        sp.wait_ge(degree_out, 16)
                        sp.dma_start(dis[:, :], deg_dram.rearrange("h l -> (h l)")
                                     .rearrange("(p b) -> p b", b=B)).then_inc(dis_in, 16)
                        sp.wait_ge(dis_in, 16)

                @block.gpsimd
                def _(pool):
                    def gather(t):
                        wait_alone(pool, edges_in[t.slot], 32 * (t.turn + 1))
                        if not t.first:
                            wait_alone(pool, tile_done[t.slot], t.turn)
                        for k in range(K):
                            pool.indirect_dma_start(
                                out=got[0:t.rows, t.slot, k, :], out_offset=None, in_=node_table,
                                in_offset=bass.IndirectOffsetOnAxis(
                                    ap=src_idx[0:t.rows, t.slot, k:k + 1], axis=0)
                            ).then_inc(gathered[t.slot], 16)

                    def regular():
                        for p in pairs(pool):
                            gather(p.gather)
                        gather(TAIL_TILE)

                    def general():
                        for t in super_tiles(pool):
                            gather(t)

                    regular_or_not(pool, regular, general)

                @block.vector
                def _(dve):
                    def regular():
                        def make_labels(p):
                            wait_alone(dve, groups_in[p.slot], 32 * (p.turn + 1))
                            nc.vector.tensor_scalar(digit[:, 0, :], edge_group[:, p.slot, 0, :], 7, None,
                                                    ALU.arith_shift_right)
                            nc.vector.tensor_scalar(digit[:, 1, :], edge_group[:, p.slot, 0, :], P - 1, None,
                                                    ALU.bitwise_and)
                            nc.vector.tensor_scalar(span_node[:, :], edge_group[:, p.slot, 1, :],
                                                    group_low[:, bass.ds(p.counted, 1)], None, ALU.subtract)
                            dve.drain()
                            nc.vector.scalar_tensor_tensor(out=label[:, p.slot, 0, :], in0=digit[:, 0, :],
                                                           scalar=float(C), in1=span_node[:, :],
                                                           op0=ALU.mult, op1=ALU.add)
                            nc.vector.tensor_copy(label[:, p.slot, 1, :], digit[:, 1, :])
                            dve.drain().then_inc(labeled, 1)

                        def take_columns(p):
                            dve.wait_ge(label_turned, p.number + 1)
                            nc.vector.tensor_copy(column[:, p.slot, :], label_ps[:, 0:2 * K])
                            dve.drain()

                        def make_pick(t):
                            wait_alone(dve, edges_in[t.slot], 32 * (t.turn + 1))
                            nc.vector.tensor_scalar(rel[0:t.rows, :], dst_idx[0:t.rows, t.slot, :],
                                                    base_all[0:t.rows, bass.ds(t.number, 1)],
                                                    window_off[0:t.rows, 0:1], ALU.subtract, ALU.subtract)
                            dve.drain()
                            nc.vector.tensor_tensor(
                                pick[0:t.rows], rel[0:t.rows, :].unsqueeze(2).to_broadcast([t.rows, K, W]),
                                iota_w[0:t.rows].unsqueeze(1).to_broadcast([t.rows, K, W]), ALU.is_equal
                            ).then_inc(pick_made, 1)

                        def window_nodes(number):
                            base = dve.value_load(windows[0:1, bass.ds(4 * number + 2, 1)],
                                                  min_val=-W * MOST, max_val=N)
                            return agg[:, bass.ds((base + W * number).with_bounds(min_val=0, max_val=NP), W)]

                        def add_gathered(number, t):
                            nodes = window_nodes(t.number)
                            dve.wait_ge(summed, number + 1)
                            nc.vector.tensor_tensor(nodes, nodes, sums[:, 0:W], ALU.add)
                            dve.drain().then_inc(tile_done[t.slot], 1)

                        def take_rows(p):
                            dve.wait_ge(multiplied, p.number + 1)
                            nc.vector.tensor_copy(pair_rows[:, :], pair_ps[:, 0:3 * D])
                            nc.vector.tensor_scalar(pair_pick[:, :], iota_w[0:CD, :],
                                                    pair_node[:, bass.ds(p.counted, 1)], None, ALU.is_equal)
                            dve.drain().then_inc(pair_rows_made, 1)

                        def add_pairs(p):
                            nodes = window_nodes(p.counted)
                            dve.wait_ge(pairs_summed, p.number + 1)
                            nc.vector.tensor_tensor(nodes, nodes, pair_sums[:, 0:W], ALU.add)
                            dve.drain()

                        left = tmp
                        for q in range(3):
                            nc.vector.tensor_copy(parts[:, :, q, :], left[:, :, :])
                            dve.drain()
                            if q < 2:
                                nc.vector.tensor_tensor(hs[:, :, :], left[:, :, :], parts[:, :, q, :],
                                                        ALU.subtract)
                                dve.drain()
                            left = hs
                        make_labels(Pair(0, 0))
                        make_pick(Pair(0, 0).gather)
                        take_columns(Pair(0, 0))
                        for p in pairs(dve):
                            if not p.last:
                                make_labels(p.next())
                            for k in range(K):
                                if not (p.start and k < ONE_HOTS):
                                    dve.wait_ge(group_counted, K * p.number + k + 1 - ONE_HOTS)
                                nc.vector.tensor_scalar(hot_pair[:, k % ONE_HOTS, :], iota_pair[:, :],
                                                        column[:, p.slot, k:k + 1], None, ALU.is_equal
                                                        ).then_inc(one_hots, 1)
                                nc.vector.tensor_scalar(hot_low[:, p.slot, k, :], iota_lo[:, :],
                                                        column[:, p.slot, K + k:K + k + 1], None, ALU.is_equal
                                                        ).then_inc(one_hots, 1)
                            add_gathered(p.number, p.gather)
                            make_pick(TAIL_TILE if p.last else p.next().gather)
                            if not p.start:
                                take_rows(p.previous())
                            if not p.last:
                                take_columns(p.next())
                            if not p.start:
                                add_pairs(p.previous())
                        add_gathered(LAST_PAIR.number + 1, TAIL_TILE)
                        take_rows(LAST_PAIR)
                        add_pairs(LAST_PAIR)

                    def general():
                        if layer == 3:
                            dve.sem_inc(target_used, 1)
                        for t in super_tiles(dve):
                            n, s = t.rows, t.slot
                            first, end, base = window_range(dve, t)
                            wait_alone(dve, edges_in[s], 32 * (t.turn + 1))
                            if layer == 1:
                                nc.vector.tensor_scalar(digit[0:n, 0, :], src_idx[0:n, s, :], 7, None,
                                                        ALU.arith_shift_right)
                                nc.vector.tensor_scalar(digit[0:n, 1, :], src_idx[0:n, s, :], P - 1, None,
                                                        ALU.bitwise_and)
                                if not (t.first and s == 0):
                                    wait_alone(dve, counted, t.number)
                                dve.drain()
                                nc.vector.tensor_tensor(
                                    hot_hi[0:n], digit[0:n, 0, :].unsqueeze(2).to_broadcast([n, K, HI]),
                                    iota_hi[0:n].unsqueeze(1).to_broadcast([n, K, HI]), ALU.is_equal)
                                nc.vector.tensor_tensor(
                                    hot_lo[0:n], digit[0:n, 1, :].unsqueeze(2).to_broadcast([n, K, P]),
                                    iota_lo[0:n].unsqueeze(1).to_broadcast([n, K, P]), ALU.is_equal)
                                dve.drain().then_inc(digits_made, 1)
                            if layer == 1:
                                dve.wait_ge(attr_in[s], 16 * (t.turn + 1))
                                dve.wait_ge(gathered[s], 16 * K * (t.turn + 1))
                                rows = got[0:n, s, :, :].rearrange("p k f -> p (k f)")
                                nc.vector.tensor_tensor(rows, rows, attr[0:n, s, :], ALU.add).then_inc(added, 1)
                            with dve.Fori(first, end) as j:
                                w = (j - first).with_bounds(min_val=0, max_val=WINDOWS - 1)
                                nc.vector.tensor_scalar(rel[0:n, :], dst_idx[0:n, s, :],
                                                        base_all[0:n, bass.ds(t.number, 1)],
                                                        window_off[0:n, bass.ds(w, 1)],
                                                        ALU.subtract, ALU.subtract)
                                dve.drain()
                                nc.vector.tensor_tensor(
                                    pick[0:n], rel[0:n, :].unsqueeze(2).to_broadcast([n, K, W]),
                                    iota_w[0:n].unsqueeze(1).to_broadcast([n, K, W]), ALU.is_equal
                                ).then_inc(pick_made, 1)
                                if layer == 3:
                                    wait_alone(dve, target_in, 16 * (j + 1))
                                    dve.drain()
                                    nc.vector.tensor_tensor(share[0:n], pick[0:n],
                                                            target[0:n].unsqueeze(1).to_broadcast([n, K, W]),
                                                            ALU.mult).then_inc(target_used, 1)
                                    dve.drain()
                                    nc.vector.tensor_reduce(logit[0:n, :], share[0:n], X, ALU.add)
                                    wait_alone(dve, gathered[s], 16 * K * (t.turn + 1))
                                    dve.drain()
                                    nc.vector.tensor_tensor(logit[0:n, :], logit[0:n, :], got[0:n, s, :, D],
                                                            ALU.add).then_inc(logits_made, 1)
                                    dve.wait_ge(gated, j + 1)
                                    nc.vector.tensor_tensor(msg[0:n], got[0:n, s, :, 0:D],
                                                            gate[0:n, :].unsqueeze(2).to_broadcast([n, K, D]),
                                                            ALU.mult).then_inc(msg_made, 1)
                                dve.wait_ge(summed, j + 1)
                                nodes = agg[:, bass.ds(first_node(base, j), W)]
                                nc.vector.tensor_tensor(nodes, nodes, sums[:, 0:W], ALU.add)
                                dve.drain()
                            dve.drain().then_inc(tile_done[s], 1)

                    regular_or_not(dve, regular, general)
                    if layer == 1:
                        dve.wait_ge(counted, TILES)
                        nc.vector.tensor_copy(degree_lo[:, :], degree[:, 0:HI]).then_inc(degree_copied, 1)
                        dve.wait_ge(degree_turned, 1)
                        nc.vector.tensor_copy(degree_hi[:, :], degree_turned_ps[0:HI, 0:P]).then_inc(turned_copied, 1)
                        dve.wait_ge(dis_in, 16)
                        nc.vector.tensor_scalar(stat[:, :], dis[:, :], 1.0, None, ALU.min)
                        nc.vector.tensor_scalar(dis[:, :], dis[:, :], 1.0, None, ALU.max
                                                ).then_inc(degree_copied, 1)
                        dve.wait_ge(turned_copied, 2)
                        nc.vector.reciprocal(dis[:, :], dis[:, :])
                        dve.drain()
                        nc.vector.tensor_tensor(dis[:, :], dis[:, :], stat[:, :], ALU.mult)

                @block.scalar
                def _(act):
                    def regular():
                        for p in pairs(act):
                            for k in range(K):
                                if k == 0 and not p.first:
                                    act.wait_ge(multiplied, p.number - 1)
                                act.wait_ge(group_counted, K * p.number + k + 1)
                                for half in (0, 1):
                                    at = (2 * (k % 2) + half) * BANK
                                    nc.scalar.copy(
                                        counts[p.slot][:, half * HALF:(half + 1) * HALF, k * C:(k + 1) * C],
                                        counts_ps[:, at:at + HALF * C].rearrange("p (h c) -> p h c", c=C)
                                    ).then_inc(counts_copied, 1)

                    if layer == 0:
                        regular_or_not(act, regular, None)
                    if layer == 1:
                        for t in super_tiles(act):
                            act.wait_ge(added, t.number + 1)
                            rows = got[0:t.rows, t.slot, :, :].rearrange("p k f -> p (k f)")
                            nc.scalar.activation(rows, rows, ACT.Relu).then_inc(rectified, 1)
                        act.wait_ge(degree_copied, 2)
                        nc.scalar.activation(dis[:, :], dis[:, :], ACT.Sqrt).then_inc(turned_copied, 1)
                    if layer == 3:
                        for t in super_tiles(act):
                            first, end = window_range(act, t, with_base=False)
                            with act.Fori(first, end) as j:
                                act.wait_ge(logits_made, j + 1)
                                nc.scalar.activation(gate[0:t.rows, :], logit[0:t.rows, :], ACT.Sigmoid
                                                     ).then_inc(gated, 1)

                @block.tensor
                def _(pe):
                    def regular():
                        def turn_labels(p):
                            wait_alone(pe, labeled, p.number + 1)
                            for q in (0, 1):
                                mm = nc.tensor.transpose(label_ps[:, q * K:(q + 1) * K],
                                                         label[:, p.slot, q, :], ident[0:K, 0:K])
                            mm.then_inc(label_turned, 1)

                        def sum_gathered(number, t):
                            wait_alone(pe, gathered[t.slot], 16 * K * (t.turn + 1))
                            pe.wait_ge(pick_made, number + 1)
                            for k in range(K):
                                mm = nc.tensor.matmul(sums[:, 0:W], got[0:t.rows, t.slot, k, 0:D],
                                                      pick[0:t.rows, k, :], start=(k == 0), stop=(k == K - 1))
                            mm.then_inc(summed, 1)

                        def count_group(p, k):
                            pe.wait_ge(one_hots, 2 * (K * p.number + k + 1))
                            if not (p.start and k < 2):
                                pe.wait_ge(counts_copied, 2 * K * p.number + 2 * k - 2)
                            for half in (0, 1):
                                at = (2 * (k % 2) + half) * BANK
                                mm = nc.tensor.matmul(
                                    counts_ps[:, at:at + HALF * C], hot_low[:, p.slot, k, :],
                                    hot_pair[:, k % ONE_HOTS, half * HALF * C:(half + 1) * HALF * C],
                                    start=True, stop=True)
                            mm.then_inc(group_counted, 1)

                        def multiply(p, high_digits):
                            for hi in high_digits:
                                if hi == 0:
                                    pe.wait_ge(counts_copied, 2 * K * (p.number + 1))
                                mm = nc.tensor.matmul(pair_ps[:, 0:3 * D], counts[p.slot][:, hi, :],
                                                      parts[:, hi, :, :].rearrange("p s f -> p (s f)"),
                                                      start=(hi == 0), stop=(hi == HI - 1),
                                                      skip_group_check=True)
                            if hi == HI - 1:
                                mm.then_inc(multiplied, 1)

                        def sum_pairs(p):
                            pe.wait_ge(pair_rows_made, p.number + 1)
                            for q in range(3):
                                mm = nc.tensor.matmul(pair_sums[:, 0:W], pair_rows[:, q * D:(q + 1) * D],
                                                      pair_pick[:, :], start=(q == 0), stop=(q == 2))
                            mm.then_inc(pairs_summed, 1)

                        turn_labels(Pair(0, 0))
                        for p in pairs(pe):
                            sum_gathered(p.number, p.gather)
                            for k in range(K):
                                count_group(p, k)
                                if not p.start:
                                    multiply(p.previous(), range(k * HI // K, (k + 1) * HI // K))
                            if not p.last:
                                turn_labels(p.next())
                            if not p.start:
                                sum_pairs(p.previous())
                        sum_gathered(LAST_PAIR.number + 1, TAIL_TILE)
                        multiply(LAST_PAIR, range(HI))
                        sum_pairs(LAST_PAIR)

                    def general():
                        for t in super_tiles(pe):
                            n, s = t.rows, t.slot
                            first, end = window_range(pe, t, with_base=False)
                            if layer == 1:
                                pe.wait_ge(digits_made, t.number + 1)
                                for k in range(K):
                                    is_first = t.first and s == 0 and k == 0
                                    mm = nc.tensor.matmul(degree[:, 0:HI], hot_lo[0:n, k, :], hot_hi[0:n, k, :],
                                                          start=is_first, stop=(n == TAIL and k == K - 1),
                                                          skip_group_check=True)
                                mm.then_inc(counted, 1)
                            if layer != 1:
                                wait_alone(pe, gathered[s], 16 * K * (t.turn + 1))
                            if layer == 1:
                                wait_alone(pe, rectified, t.number + 1)
                            with pe.Fori(first, end) as j:
                                pe.wait_ge(pick_made, j + 1)
                                if layer == 3:
                                    pe.wait_ge(msg_made, j + 1)
                                for k in range(K):
                                    rows = msg[0:n, k, :] if layer == 3 else got[0:n, s, k, 0:D]
                                    mm = nc.tensor.matmul(sums[:, 0:W], rows, pick[0:n, k, :],
                                                          start=(k == 0), stop=(k == K - 1))
                                mm.then_inc(summed, 1)

                    regular_or_not(pe, regular, general)
                    if layer == 1:
                        pe.wait_ge(degree_copied, 1)
                        nc.tensor.transpose(degree_turned_ps[0:HI, 0:P], degree_lo[:, :], ident[:, :]
                                            ).then_inc(degree_turned, 1)

        def sum_by_src():
            with ExitStack() as ph:
                sem = lambda name: ph.enter_context(nc.semaphore(f"{name}2"))
                buf = lambda name, shape, dt=F32: sb(f"{name}2", shape, dt, ph)
                psum = lambda name, shape: ph.enter_context(nc.psum_tensor(f"{name}2", shape, F32))
                src_idx = buf("src_idx", [P, 2, K], I32)
                src_f = buf("src_f", [P, 2, K])
                weight = buf("weight", [P, 2, K])
                src_all = buf("src_all", [P, 2, SUPER], I32)
                dst_all = buf("dst_all", [W, 2, SUPER], I32)
                window_rows = buf("window_rows", [W, D])
                pick = buf("pick", [W, SUPER])
                rows = buf("rows", [P, K, DR])
                same = buf("same", [P, 2, K, P])
                zero_row = buf("zero_row", [1, BANK], BF16)
                dup = buf("dup", [P, K])
                to_dump = buf("to_dump", [P, 2, K])
                target = buf("target", [P, 2, K], I32)
                totals = buf("totals", [P, 2, K, D])
                rows_ps = psum("rows_ps", [P, BANK])
                totals_ps = psum("totals_ps", [P, BANK])
                edges_in = [sem(f"edges_in{s}_") for s in (0, 1)]
                tile_done = [sem(f"tile_done{s}_") for s in (0, 1)]
                scattered = [sem(f"scattered{r}_") for r in range(R)]
                window_in, pick_made, expanded, rows_made, totaled, totals_copied, targets_made, zero_made = (
                    sem("window_in"), sem("pick_made"), sem("expanded"), sem("rows_made"),
                    sem("totaled"), sem("totals_copied"), sem("targets_made"), sem("zero_made"))
                block = ph.enter_context(nc.Block())

                @block.sync
                def _(sp):
                    for t in super_tiles(sp):
                        if not t.first:
                            sp.wait_ge(tile_done[t.slot], t.turn)
                        n, s = t.rows, t.slot
                        first, end, base = window_range(sp, t)
                        sp.dma_start(src_idx[0:n, s, :], edge_rows(src_rows, t)).then_inc(edges_in[s], 16)
                        sp.dma_start(weight[0:n, s, :], edge_rows(weight_rows, t)).then_inc(edges_in[s], 16)
                        for values, where, parts in ((src, src_all, P), (dst, dst_all, W)):
                            sp.dma_start(where[:, s, 0:n * K],
                                         values.rearrange("(a e) -> a e", a=1)
                                         [:, bass.ds(t.number * SUPER, n * K)].to_broadcast([parts, n * K])
                                         ).then_inc(edges_in[s], 16)
                        with sp.Fori(first, end) as j:
                            sp.wait_ge(expanded, j + 1)
                            sp.dma_start(window_rows[:, :], x2_dram[bass.ds(first_node(base, j), W), :]
                                         ).then_inc(window_in, 16)

                @block.vector
                def _(dve):
                    nc.vector.memset(zero_row[:, :], 0.0).then_inc(zero_made, 1)
                    nc.vector.tensor_copy(rows[:, :, D], rank[:, 0:1].to_broadcast([P, K]))

                    def name_targets(number, n, s):
                        dve.wait_ge(totals_copied, number + 1)
                        nc.vector.tensor_scalar(
                            dup[0:n, :], totals_ps[0:n, 0:K * DR].rearrange("p (k f) -> p k f", k=K)[:, :, D],
                            rank[0:n, 1:2], None, ALU.is_gt)
                        dve.drain()
                        nc.vector.tensor_tensor(dup[0:n, :], dup[0:n, :], to_dump[0:n, s, :], ALU.mult)
                        dve.drain()
                        nc.vector.tensor_tensor(target[0:n, s, :], dup[0:n, :], src_f[0:n, s, :], ALU.add)
                        dve.drain().then_inc(targets_made, 1)

                    for t in super_tiles(dve):
                        n, s = t.rows, t.slot
                        first, end = window_range(dve, t, with_base=False)
                        wait_alone(dve, edges_in[s], 64 * (t.turn + 1))
                        with dve.Fori(first, end) as j:
                            w = (j - first).with_bounds(min_val=0, max_val=WINDOWS - 1)
                            dve.wait_ge(expanded, j + 1)
                            nc.vector.tensor_scalar(pick[:, 0:n * K], dst_all[:, s, 0:n * K],
                                                    base_all[0:W, bass.ds(t.number, 1)],
                                                    window_node[0:W, bass.ds(w, 1)],
                                                    ALU.subtract, ALU.is_equal).then_inc(pick_made, 1)
                        nc.vector.tensor_copy(src_f[0:n, s, :], src_idx[0:n, s, :])
                        nc.vector.tensor_scalar(to_dump[0:n, s, :], src_idx[0:n, s, :], -1.0,
                                                dump_row[0:n, :], ALU.mult, ALU.add)
                        dve.drain()
                        edge = src_all[0:n, s, 0:n * K].rearrange("p (r k) -> p k r", k=K)
                        for k in range(K):
                            nc.vector.tensor_scalar(same[0:n, s, k, 0:n], edge[:, k, :],
                                                    src_f[0:n, s, k:k + 1], None, ALU.is_equal)
                        if not (t.first and s == 0):
                            name_targets(t.number - 1, P, 1 - s)
                        dve.wait_ge(expanded, end + 1)
                        nc.vector.tensor_tensor(
                            rows[0:n, :, 0:D], rows_ps[0:n, 0:K * D].rearrange("p (k f) -> p k f", k=K),
                            weight[0:n, s, :].unsqueeze(2).to_broadcast([n, K, D]), ALU.mult)
                        dve.drain().then_inc(rows_made, 1)
                        dve.sem_inc(tile_done[s], 1)
                    name_targets(TILES - 1, TAIL, 0)

                @block.tensor
                def _(pe):
                    pe.sem_inc(expanded, 1)
                    pe.wait_ge(zero_made, 1)
                    for t in super_tiles(pe):
                        n = t.rows
                        first, end = window_range(pe, t, with_base=False)
                        nc.tensor.matmul(rows_ps[:, :], zero_row[:, 0:P], zero_row[:, :], start=True,
                                         stop=False, skip_group_check=True)
                        with pe.Fori(first, end) as j:
                            pe.wait_ge(pick_made, j + 1)
                            pe.wait_ge(window_in, 16 * (j + 1))
                            for k in range(K):
                                mm = nc.tensor.matmul(
                                    rows_ps[0:n, k * D:(k + 1) * D],
                                    pick[:, 0:n * K].rearrange("w (r k) -> w k r", k=K)[:, k, :],
                                    window_rows[:, :], start=False, stop=(k == K - 1), skip_group_check=True)
                            mm.then_inc(expanded, 1)
                        pe.wait_ge(rows_made, t.number + 1)
                        if not (t.first and t.slot == 0):
                            pe.wait_ge(totals_copied, t.number)
                        for k in range(K):
                            mm = nc.tensor.matmul(totals_ps[0:n, k * DR:(k + 1) * DR],
                                                  same[0:n, t.slot, k, 0:n], rows[0:n, k, :],
                                                  start=True, stop=True)
                        mm.then_inc(totaled, 1)

                @block.scalar
                def _(act):
                    for t in super_tiles(act):
                        act.wait_ge(totaled, t.number + 1)
                        if not t.first:
                            for r in range(R):
                                act.wait_ge(scattered[r], 16 * (K // R) * (t.number - 1))
                        nc.scalar.copy(totals[0:t.rows, t.slot, :, :],
                                       totals_ps[0:t.rows, 0:K * DR].rearrange("p (k f) -> p k f", k=K)
                                       [:, :, 0:D]).then_inc(totals_copied, 1)

                @block.gpsimd
                def _(pool):
                    for t in super_tiles(pool):
                        n, s = t.rows, t.slot
                        wait_alone(pool, totals_copied, t.number + 1)
                        wait_alone(pool, targets_made, t.number + 1)
                        for k in range(K):
                            r, turn = k % R, k // R
                            if not (t.first and s == 0 and turn == 0):
                                wait_alone(pool, scattered[r], 16 * ((K // R) * t.number + turn))
                            pool.indirect_dma_start(
                                out=z_dram[r],
                                out_offset=bass.IndirectOffsetOnAxis(ap=target[0:n, s, k:k + 1], axis=0),
                                in_=totals[0:n, s, k, :], in_offset=None,
                                compute_op=ALU.add).then_inc(scattered[r], 16)
                    for r in range(R):
                        pool.wait_ge(scattered[r], 16 * (K // R) * TILES)

        def node_phase(layer):
            with ExitStack() as ph:
                sem = lambda name: ph.enter_context(nc.semaphore(f"{name}_n{layer}"))
                buf = lambda name, shape, dt=F32: sb(f"{name}_n{layer}", shape, dt, ph)
                banks = ph.enter_context(nc.psum_tensor(f"banks{layer}", [P, 8, BANK], F32))
                node_grid = banks[:, :, :].rearrange("p c n -> p (c n)")[:, 0:B * D].rearrange(
                    "p (b f) -> p b f", f=D)
                turned, centred, rooted, tabled = sem("turned"), sem("centred"), sem("rooted"), sem("tabled")
                ready, stored = sem("ready"), sem("stored")
                inner_turned, inner_copied, hidden, rectified, projected = (
                    sem("inner_turned"), sem("inner_copied"), sem("hidden"), sem("rectified"),
                    sem("projected"))
                params_in, inner_made, parts_in = sem("params_in"), sem("inner_made"), sem("parts_in")
                G = 4
                groups = [range(b, min(b + G, B)) for b in range(0, B, G)]
                inner = buf("inner", [D, 2, G * P])
                inner2 = buf("inner2", [D, 2, G * P])
                evacuated = sem("evacuated")
                if layer == 1:
                    w1_row, w2_row = buf("w1_row", [D, D]), buf("w2_row", [D, D])
                    wt = buf("wt", [D, 2, D])
                    b1_col, b2_all, scale = buf("b1_col", [D, 1]), buf("b2_all", [P, D]), buf("scale", [P, 1])
                    PARAMS = 5
                if layer == 2:
                    wt = buf("wt", [D, 2, D])
                    parts = buf("parts", [P, R - 1, B * D])
                    PARAMS = 1
                if layer == 2:
                    y = buf("y", [P, B, YC])
                    vec_src, vec_tgt, bias = buf("vec_src", [P, D]), buf("vec_tgt", [P, D]), buf("bias", [P, 1])
                    target = buf("target", [P, B])
                    PARAMS += 3
                block = ph.enter_context(nc.Block())
                last_layer = L - 1

                @block.sync
                def _(sp):
                    row = lambda v: v.rearrange("(a n) -> a n", a=1)
                    if layer == 1:
                        sp.dma_start(w1_row[:, :], w1[last_layer, :, :]).then_inc(params_in, 16)
                        sp.dma_start(w2_row[:, :], w2[last_layer, :, :]).then_inc(params_in, 16)
                        sp.dma_start(b1_col[:, :], b1[last_layer, :].rearrange("(n a) -> n a", a=1)
                                     ).then_inc(params_in, 16)
                        sp.dma_start(b2_all[:, :], b2[last_layer:last_layer + 1, :].to_broadcast([P, D])
                                     ).then_inc(params_in, 16)
                        sp.dma_start(scale[:, :], row(eps)[:, last_layer:last_layer + 1].to_broadcast([P, 1])
                                     ).then_inc(params_in, 16)
                    if layer == 2:
                        sp.dma_start(wt[:, 0, :], w_lin).then_inc(params_in, 16)
                        sp.dma_start(vec_src[:, :], row(w_src).to_broadcast([P, D])).then_inc(params_in, 16)
                        sp.dma_start(vec_tgt[:, :], row(w_tgt).to_broadcast([P, D])).then_inc(params_in, 16)
                        sp.dma_start(bias[:, :], row(gate_bias).to_broadcast([P, 1])).then_inc(params_in, 16)
                        sp.dma_start(hs[:, :, :].rearrange("p b f -> p (b f)"), node_rows(z_dram[0])
                                     ).then_inc(parts_in, 16)
                        for r in range(1, R):
                            sp.dma_start(parts[:, r - 1, :], node_rows(z_dram[r])).then_inc(parts_in, 16)
                    sp.wait_ge(ready, 1)
                    flat = xs[:, :, :].rearrange("p b f -> p (b f)")
                    if layer < 2:
                        sp.dma_start(node_rows((x1_dram, x2_dram)[layer]), flat).then_inc(stored, 16)
                        sp.wait_ge(stored, 16)
                    if layer == 2:
                        sp.dma_start(node_rows(y_dram), y[:, :, :].rearrange("p b f -> p (b f)")
                                     ).then_inc(stored, 16)
                        sp.dma_start(b_dram[0:NP, :].rearrange("(p b) q -> p (b q)", b=B), target[:, :]
                                     ).then_inc(stored, 16)
                        sp.wait_ge(stored, 32)
                    if layer == 3:
                        sp.dma_start(out[0:(P - 1) * B, :].rearrange("(p b) f -> p (b f)", b=B),
                                     flat[0:P - 1, :]).then_inc(stored, 16)
                        sp.dma_start(out[(P - 1) * B:N, :].rearrange("(p b) f -> p (b f)", b=LASTROWS),
                                     flat[P - 1:P, 0:LASTROWS * D]).then_inc(stored, 16)
                        sp.wait_ge(stored, 32)

                @block.tensor
                def _(pe):
                    if layer == 1:
                        pe.wait_ge(params_in, 16 * PARAMS)
                        nc.tensor.transpose(banks[0:D, 7, 0:D], w1_row[:, :], ident[0:D, 0:D])
                        nc.tensor.transpose(banks[0:D, 7, D:2 * D], w2_row[:, :], ident[0:D, 0:D]
                                            ).then_inc(tabled, 1)
                    if layer != 2:
                        by_block = agg[:, 0:NP].rearrange("f (p b) -> f b p", b=B)
                        for b in range(B):
                            mm = nc.tensor.transpose(node_grid[:, b, :], by_block[:, b, :], ident[0:D, 0:D])
                        mm.then_inc(turned, 1)
                    if layer in (1, 2):
                        pe.wait_ge(inner_made, 1)
                        if layer == 1:
                            pe.wait_ge(tabled, 2)

                        def turn(g):
                            for q, b in enumerate(groups[g]):
                                mm = nc.tensor.transpose(banks[0:D, g % 2, q * P:(q + 1) * P],
                                                         hs[:, b, :], ident[:, :])
                            mm.then_inc(inner_turned, 1)

                        def project(g):
                            if layer == 1:
                                pe.wait_ge(rectified, g + 1)
                            if g >= 4:
                                pe.wait_ge(evacuated, g - 3)
                            last = inner2 if layer == 1 else inner
                            for q, b in enumerate(groups[g]):
                                mm = nc.tensor.matmul(banks[:, 4 + g % 4, q * D:(q + 1) * D],
                                                      last[:, g % 2, q * P:(q + 1) * P],
                                                      wt[:, 1 if layer == 1 else 0, :], start=True, stop=True)
                            mm.then_inc(projected, 1)

                        turn(0)
                        for g in range(len(groups)):
                            if g + 1 < len(groups):
                                turn(g + 1)
                            pe.wait_ge(inner_copied, g + 1)
                            if layer == 1:
                                n = len(groups[g]) * P
                                nc.tensor.matmul(banks[0:D, 2 + g % 2, 0:n], wt[:, 0, :],
                                                 inner[:, g % 2, 0:n], start=True, stop=True
                                                 ).then_inc(hidden, 1)
                                if g >= 1:
                                    project(g - 1)
                            else:
                                project(g)
                        if layer == 1:
                            project(len(groups) - 1)

                @block.scalar
                def _(act):
                    def copy_rows(g):
                        act.wait_ge(inner_turned, g + 1)
                        if layer == 2 and g >= 2:
                            act.wait_ge(projected, g - 1)
                        n = len(groups[g]) * P
                        nc.scalar.copy(inner[:, g % 2, 0:n], banks[0:D, g % 2, 0:n]).then_inc(inner_copied, 1)

                    if layer == 2:
                        for g in range(len(groups)):
                            copy_rows(g)
                    if layer == 1:
                        copy_rows(0)
                        for g in range(len(groups)):
                            if g + 1 < len(groups):
                                copy_rows(g + 1)
                            act.wait_ge(hidden, g + 1)
                            if g >= 2:
                                act.wait_ge(projected, g - 1)
                            n = len(groups[g]) * P
                            nc.scalar.activation(inner2[:, g % 2, 0:n], banks[0:D, 2 + g % 2, 0:n], ACT.Relu,
                                                 bias=b1_col[:, :]).then_inc(rectified, 1)
                    act.wait_ge(centred, 1)
                    nc.scalar.activation(stat[:, :], stat[:, :], ACT.Sqrt, bias=eps_col[:, :], scale=1.0 / D
                                         ).then_inc(rooted, 1)

                @block.vector
                def _(dve):
                    across = lambda v: v.unsqueeze(2).to_broadcast([P, B, D])
                    along = lambda v: v.unsqueeze(1).to_broadcast([P, B, D])
                    if layer == 1:
                        dve.wait_ge(tabled, 1)
                        nc.vector.tensor_copy(wt[:, :, :].rearrange("f a g -> f (a g)"),
                                              banks[0:D, 7, 0:2 * D]).then_inc(tabled, 1)
                        nc.vector.tensor_scalar(scale[:, :], scale[:, :], 1.0, None, ALU.add)
                        dve.wait_ge(turned, 1)
                        dve.drain()
                        nc.vector.scalar_tensor_tensor(
                            out=hs[:, :, :], in0=xs[:, :, :], scalar=scale[:, :],
                            in1=node_grid, op0=ALU.mult, op1=ALU.add)
                        dve.drain().then_inc(inner_made, 1)
                        nc.vector.memset(agg[:, :], 0.0)
                        for g, blocks in enumerate(groups):
                            dve.wait_ge(projected, g + 1)
                            n = len(blocks)
                            nc.vector.tensor_tensor(
                                hs[:, blocks[0]:blocks[0] + n, :], b2_all[:, :].unsqueeze(1).to_broadcast([P, n, D]),
                                banks[:, 4 + g % 4, 0:n * D].rearrange("p (b f) -> p b f", f=D), ALU.add
                            ).then_inc(evacuated, 1)
                        dve.drain()
                        nc.vector.tensor_scalar(hs[:, :, :], hs[:, :, :], 0.0, None, ALU.max)
                        dve.drain()
                        nc.vector.tensor_tensor(xs[:, :, :], xs[:, :, :], hs[:, :, :], ALU.add)
                    if layer == 2:
                        flat = hs[:, :, :].rearrange("p b f -> p (b f)")
                        dve.wait_ge(parts_in, 16 * R)
                        for r in range(1, R):
                            nc.vector.tensor_tensor(flat, flat, parts[:, r - 1, :], ALU.add)
                            dve.drain()
                        dve.sem_inc(inner_made, 1)
                        for g, blocks in enumerate(groups):
                            dve.wait_ge(projected, g + 1)
                            rows = xs[:, blocks[0]:blocks[-1] + 1, :]
                            nc.vector.tensor_tensor(
                                rows, rows, banks[:, 4 + g % 4, 0:len(blocks) * D].rearrange(
                                    "p (b f) -> p b f", f=D), ALU.add).then_inc(evacuated, 1)
                    if layer == 3:
                        dve.wait_ge(turned, 1)
                        nc.vector.tensor_tensor(hs[:, :, :], across(dis[:, :]), node_grid, ALU.mult)
                        dve.drain()
                        nc.vector.tensor_tensor(xs[:, :, :], xs[:, :, :], hs[:, :, :], ALU.add)
                    if layer == 0:
                        dve.wait_ge(turned, 1)
                        nc.vector.tensor_tensor(xs[:, :, :], xs[:, :, :], node_grid, ALU.add)
                    dve.drain()
                    if layer == 0:
                        nc.vector.memset(agg[:, :], 0.0)
                    nc.vector.tensor_reduce(stat[:, :], xs[:, :, :], X, ALU.add)
                    dve.drain()
                    nc.vector.tensor_scalar(stat[:, :], stat[:, :], 1.0 / D, None, ALU.mult)
                    dve.drain()
                    nc.vector.tensor_tensor(xs[:, :, :], xs[:, :, :], across(stat[:, :]), ALU.subtract)
                    dve.drain()
                    nc.vector.tensor_tensor(tmp[:, :, :], xs[:, :, :], xs[:, :, :], ALU.mult)
                    dve.drain()
                    nc.vector.tensor_reduce(stat[:, :], tmp[:, :, :], X, ALU.add).then_inc(centred, 1)
                    dve.wait_ge(rooted, 1)
                    nc.vector.reciprocal(stat[:, :], stat[:, :])
                    dve.drain()
                    nc.vector.tensor_tensor(xs[:, :, :], xs[:, :, :], across(stat[:, :]), ALU.mult)
                    dve.drain()
                    if layer == 2:
                        dve.wait_ge(params_in, 16 * PARAMS)
                        nc.vector.memset(y[:, :, D:YC], 0.0)
                        nc.vector.tensor_tensor(y[:, :, 0:D], xs[:, :, :], across(dis[:, :]), ALU.mult)
                        nc.vector.tensor_tensor(tmp[:, :, :], xs[:, :, :], along(vec_src[:, :]), ALU.mult)
                        nc.vector.tensor_tensor(hs[:, :, :], xs[:, :, :], along(vec_tgt[:, :]), ALU.mult)
                        dve.drain()
                        nc.vector.tensor_reduce(y[:, :, D], tmp[:, :, :], X, ALU.add)
                        nc.vector.tensor_reduce(target[:, :], hs[:, :, :], X, ALU.add)
                        dve.drain()
                        nc.vector.tensor_scalar(target[:, :], target[:, :], bias[:, :], None, ALU.add)
                    dve.drain().then_inc(ready, 1)

        sum_by_dst(0)
        node_phase(0)
        sum_by_dst(1)
        node_phase(1)
        sum_by_src()
        node_phase(2)
        sum_by_dst(3)
        node_phase(3)


_INS = ["x", "src", "dst", "edge_attr_32", "edge_weight", "L1_gnn_eps", "L1_gnn_W1", "L1_gnn_b1",
        "L1_gnn_W2", "L1_gnn_b2", "L2_gnn_weight", "L3_gnn_w_src", "L3_gnn_w_tgt", "L3_gnn_gate_bias"]


def kernel(**inputs):
    import numpy as np
    import concourse.bacc as bacc
    from concourse.bass_utils import run_bass_kernel_spmd

    nc = bacc.Bacc("TRN2", target_bir_lowering=False, num_devices=1)
    arrays, args = {}, []
    for name in _INS:
        a = np.ascontiguousarray(inputs[name])
        arrays[name] = a
        args.append(nc.dram_tensor(name, a.shape, mybir.dt.from_np(a.dtype), kind="ExternalInput").ap())
    n, d = inputs["x"].shape
    args.append(nc.dram_tensor("out", (n, d), F32, kind="ExternalOutput").ap())
    build_program(nc, *args)
    result = run_bass_kernel_spmd(nc, [arrays], core_ids=[0])
    return result.results[0]["out"]
```
